# Optimizing a Trainium2 kernel written in Bass

```python
import numpy as np
import jax
import jax.numpy as jnp

def _softmax(x, axis=-1):
    return jax.nn.softmax(x, axis=axis)

def _gelu(x):
    return jax.nn.gelu(x, approximate=True)

def _silu(x):
    return jax.nn.silu(x)

def _sigmoid(x):
    return jax.nn.sigmoid(x)

def _layernorm(x, axis=-1, eps=1e-05):
    m = jnp.mean(x, axis=axis, keepdims=True)
    v = jnp.var(x, axis=axis, keepdims=True)
    return (x - m) / jnp.sqrt(v + eps)

def _scatter_add(tgt, idx, src, axis=0):
    return tgt.at[idx].add(src)

def _segment_sum(src, seg, n):
    return jax.ops.segment_sum(src, seg, n)
kernel_name = 'mk_adj_preln_d4_adj_r2_c3cbf2'

def setup_inputs(seed: int=0):
    np.random.seed(seed)
    _w = jnp.asarray

    def _rec_inputs():
        import jax
        import jax.numpy as jnp
        _gk = jax.random.key(seed)
        x = 7.22e-05 + 1 * jax.random.normal(jax.random.fold_in(_gk, 1), (64, 128, 256), jnp.float32)
        _w = (1.0 + jnp.arange(128, dtype=jnp.float32)) ** (-0.5)
        _w = _w / _w.mean()
        _pij = jnp.clip(0.125 * _w[:, None] * _w[None, :], 0.0, 1.0)
        _a = jax.random.uniform(jax.random.fold_in(_gk, 2), (128, 128)) < _pij
        _af = _a.astype(jnp.float32)
        adj = _af
        return (x, adj)
    x, adj = _rec_inputs()

    def _L0_gnn_setup():
        import jax, jax.numpy as jnp
        import numpy as np
        B, N, D = (8, 1024, 256)
        key = jax.random.key(seed)
        k1, k2, k3, k4, k5 = jax.random.split(key, 5)
        neuron_states = jax.random.normal(k1, (B, N, D), dtype=jnp.float32)
        adjacency = jax.random.randint(k2, (N, N), 0, 2).astype(jnp.float32)
        scale = 1.0 / np.sqrt(D)
        Wq = jax.random.normal(k3, (D, D), dtype=jnp.float32) * scale
        Wk = jax.random.normal(k4, (D, D), dtype=jnp.float32) * scale
        Wv = jax.random.normal(k5, (D, D), dtype=jnp.float32) * scale
        return {'neuron_states': neuron_states, 'adjacency': adjacency, 'Wq': Wq, 'Wk': Wk, 'Wv': Wv}
    _L0_gnn_all = _L0_gnn_setup()
    _L0_gnn_in = {k: v for k, v in _L0_gnn_all.items() if k in ('Wq', 'Wk', 'Wv')}
    del _L0_gnn_all

    def _L1_gnn_setup():
        import jax, jax.numpy as jnp
        import numpy as np
        ALPHA = 0.2
        key = jax.random.key(seed)
        k0, k1, k2, k3 = jax.random.split(key, 4)
        B, N, C, F = (64, 512, 256, 256)
        x = jax.random.normal(k0, (B, N, C), dtype=jnp.float32)
        W = jax.random.normal(k1, (C, F), dtype=jnp.float32) * (1.414 / np.sqrt(C + F))
        a = jax.random.normal(k2, (2 * F, 1), dtype=jnp.float32) * (1.414 / np.sqrt(2 * F + 1))
        beta = jnp.ones((1,), dtype=jnp.float32)
        mask = (jax.random.uniform(k3, (N, N)) < 0.3).astype(jnp.float32)
        return {'x': x, 'W': W, 'a': a, 'beta': beta, 'mask': mask}
    _L1_gnn_all = _L1_gnn_setup()
    _L1_gnn_in = {k: v for k, v in _L1_gnn_all.items() if k in ('W', 'a', 'beta')}
    del _L1_gnn_all

    def _L2_gnn_setup():
        import jax, jax.numpy as jnp
        import numpy as np
        B, N, F_IN, F_OUT = (16, 1024, 256, 256)
        key = jax.random.key(seed)
        k1, k2, k3 = jax.random.split(key, 3)
        x = jax.random.normal(k1, (B, N, F_IN), dtype=jnp.float32)
        adj = jax.random.uniform(k2, (N, N), dtype=jnp.float32)
        bound = np.sqrt(6.0 / F_OUT)
        weight = jax.random.uniform(k3, (F_IN, F_OUT), dtype=jnp.float32, minval=-bound, maxval=bound)
        bias = jnp.zeros((F_OUT,), dtype=jnp.float32)
        return {'x': x, 'adj': adj, 'weight': weight, 'bias': bias}
    _L2_gnn_all = _L2_gnn_setup()
    _L2_gnn_in = {k: v for k, v in _L2_gnn_all.items() if k in ('weight', 'bias')}
    del _L2_gnn_all

    def _L3_gnn_setup():
        import jax, jax.numpy as jnp
        import numpy as np
        B, N, D, H = (4, 1024, 256, 8)
        HD = D // H
        key = jax.random.key(seed)
        ks = jax.random.split(key, 10)
        x = jax.random.normal(ks[0], (B, N, D), dtype=jnp.float32)
        adj = (jax.random.uniform(ks[1], (N, N)) < 0.1).astype(jnp.float32)
        s = 1.0 / np.sqrt(D)
        Wq = jax.random.normal(ks[2], (D, D), dtype=jnp.float32) * s
        Wk = jax.random.normal(ks[3], (D, D), dtype=jnp.float32) * s
        Wv = jax.random.normal(ks[4], (D, D), dtype=jnp.float32) * s
        Wo = jax.random.normal(ks[5], (D, D), dtype=jnp.float32) * s
        bq = jnp.zeros((D,), jnp.float32)
        bk = jnp.zeros((D,), jnp.float32)
        bv = jnp.zeros((D,), jnp.float32)
        bo = jnp.zeros((D,), jnp.float32)
        return {'x': x, 'adj': adj, 'Wq': Wq, 'bq': bq, 'Wk': Wk, 'bk': bk, 'Wv': Wv, 'bv': bv, 'Wo': Wo, 'bo': bo}
    _L3_gnn_all = _L3_gnn_setup()
    _L3_gnn_in = {k: v for k, v in _L3_gnn_all.items() if k in ('Wq', 'bq', 'Wk', 'bk', 'Wv', 'bv', 'Wo', 'bo')}
    del _L3_gnn_all
    return {'x': x, 'adj': adj, 'L0_gnn_Wq': _L0_gnn_in['Wq'], 'L0_gnn_Wk': _L0_gnn_in['Wk'], 'L0_gnn_Wv': _L0_gnn_in['Wv'], 'L1_gnn_W': _L1_gnn_in['W'], 'L1_gnn_a': _L1_gnn_in['a'], 'L1_gnn_beta': _L1_gnn_in['beta'], 'L2_gnn_weight': _L2_gnn_in['weight'], 'L2_gnn_bias': _L2_gnn_in['bias'], 'L3_gnn_Wq': _L3_gnn_in['Wq'], 'L3_gnn_bq': _L3_gnn_in['bq'], 'L3_gnn_Wk': _L3_gnn_in['Wk'], 'L3_gnn_bk': _L3_gnn_in['bk'], 'L3_gnn_Wv': _L3_gnn_in['Wv'], 'L3_gnn_bv': _L3_gnn_in['bv'], 'L3_gnn_Wo': _L3_gnn_in['Wo'], 'L3_gnn_bo': _L3_gnn_in['bo']}

def reference(x, adj, L0_gnn_Wq, L0_gnn_Wk, L0_gnn_Wv, L1_gnn_W, L1_gnn_a, L1_gnn_beta, L2_gnn_weight, L2_gnn_bias, L3_gnn_Wq, L3_gnn_bq, L3_gnn_Wk, L3_gnn_bk, L3_gnn_Wv, L3_gnn_bv, L3_gnn_Wo, L3_gnn_bo):
    import jax
    import jax.numpy as jnp

    def _L0_gnn_ref(neuron_states, adjacency, Wq, Wk, Wv):
        import jax, jax.numpy as jnp
        import numpy as np
        B, N, D = (8, 1024, 256)
        q = jnp.einsum('bnd,ed->bne', neuron_states, Wq)
        k = jnp.einsum('bnd,ed->bne', neuron_states, Wk)
        v = jnp.einsum('bnd,ed->bne', neuron_states, Wv)
        rel = jnp.einsum('bnd,bmd->bnm', q, k)
        rel = adjacency.T[None, :, :] * rel
        rel = rel / jnp.linalg.norm(rel, axis=2, keepdims=True)
        return jnp.einsum('bnm,bmd->bnd', rel, v)

    def _L1_gnn_ref(x, W, a, beta, mask):
        import jax, jax.numpy as jnp
        import numpy as np
        ALPHA = 0.2
        F_ = W.shape[1]
        h = jnp.einsum('bnc,cf->bnf', x, W)
        a1, a2 = (a[:F_, 0], a[F_:, 0])
        s1 = jnp.einsum('bnf,f->bn', h, a1)
        s2 = jnp.einsum('bnf,f->bn', h, a2)
        e = jax.nn.leaky_relu(s1[:, :, None] + s2[:, None, :], negative_slope=ALPHA)
        e = e * mask[None, :, :]
        att = jax.nn.softmax(e, axis=2)
        h_prime = jnp.einsum('bij,bjf->bif', att, h)
        return jax.nn.elu(h_prime + beta * h)

    def _L2_gnn_ref(x, adj, weight, bias):
        import jax, jax.numpy as jnp
        import numpy as np
        B, N, F_IN, F_OUT = (16, 1024, 256, 256)
        deg = adj.sum(axis=1)
        deg_inv_sqrt = jnp.where(deg > 0, jax.lax.rsqrt(deg), 0.0)
        norm_adj = adj * deg_inv_sqrt[:, None] * deg_inv_sqrt[None, :]
        support = jnp.einsum('bni,io->bno', x, weight)
        output = jnp.einsum('nm,bmo->bno', norm_adj, support)
        return output + bias

    def _L3_gnn_ref(x, adj, Wq, bq, Wk, bk, Wv, bv, Wo, bo):
        import jax, jax.numpy as jnp
        import numpy as np
        B, N, D, H = (4, 1024, 256, 8)
        HD = D // H
        b, n, d = x.shape
        q = (x @ Wq + bq).reshape(b, n, H, HD)
        k = (x @ Wk + bk).reshape(b, n, H, HD)
        v = (x @ Wv + bv).reshape(b, n, H, HD)
        scores = jnp.einsum('bqhd,bkhd->bhqk', q, k) / jnp.sqrt(jnp.float32(HD))
        scores = scores + (1.0 - adj)[None, None, :, :] * -1000000000.0
        attn = jax.nn.softmax(scores, axis=-1)
        out = jnp.einsum('bhqk,bkhd->bqhd', attn, v).reshape(b, n, d)
        return out @ Wo + bo
    h = jnp.maximum(_layernorm(x, axis=-1), 0.0)
    x = x + _L0_gnn_ref(h, adj, L0_gnn_Wq, L0_gnn_Wk, L0_gnn_Wv)
    h = jnp.maximum(_layernorm(x, axis=-1), 0.0)
    x = x + _L1_gnn_ref(h, L1_gnn_W, L1_gnn_a, L1_gnn_beta, adj)
    h = jnp.maximum(_layernorm(x, axis=-1), 0.0)
    x = x + _L2_gnn_ref(h, adj, L2_gnn_weight, L2_gnn_bias)
    h = jnp.maximum(_layernorm(x, axis=-1), 0.0)
    x = x + _L3_gnn_ref(h, adj, L3_gnn_Wq, L3_gnn_bq, L3_gnn_Wk, L3_gnn_bk, L3_gnn_Wv, L3_gnn_bv, L3_gnn_Wo, L3_gnn_bo)
    return x

_drawn_inputs = setup_inputs


def setup_inputs(seed=0):
    import zlib

    import numpy as np

    out = dict(_drawn_inputs(seed))
    spreads = {'L2_gnn_bias': (0.0, 0.1),
     'L3_gnn_bq': (0.0, 0.8),
     'L3_gnn_bk': (0.0, 0.8),
     'L3_gnn_bv': (0.0, 0.1),
     'L3_gnn_bo': (0.0, 0.1)}
    factors = {'L1_gnn_a': 6.414}
    for name, (base, spread) in spreads.items():
        noise = np.random.default_rng([zlib.crc32(name.encode()), seed]).standard_normal(out[name].shape)
        drawn = base * np.exp(spread * noise) if base else spread * noise
        out[name] = jnp.asarray(drawn.astype(out[name].dtype))
    for name, factor in factors.items():
        out[name] = (out[name] * factor).astype(out[name].dtype)
    return out
```

```python
from contextlib import ExitStack

import numpy as np

import concourse.bass as bass
from concourse import mybir

F32 = mybir.dt.float32
ALU = mybir.AluOpType
ACT = mybir.ActivationFunctionType
AX_X = mybir.AxisListType.X


def gnn_stack_kernel(nc, x, adj, w):
    GRAPHS, N, D = x.shape
    PAIRS = GRAPHS // 2
    C = D // 128
    HEADS = 8
    HD = D // HEADS
    R = 128 // HD
    EPS = 1e-5
    ALPHA = 0.2
    QSCALE = float(HD) ** -0.5
    out = w["out"]
    assert N == 128 and C == 2 and HD == 32 and GRAPHS % 2 == 0

    with ExitStack() as ctx:
        def sb(name, shape, dt=F32):
            return ctx.enter_context(nc.sbuf_tensor(name, shape, dt))

        def sem(name):
            return ctx.enter_context(nc.semaphore(name))

        bank = [ctx.enter_context(nc.psum_tensor(f"bank{i}", [128, 512], F32)) for i in range(8)]

        xs = sb("xs", [128, GRAPHS, D])
        ident = sb("ident", [128, 128])
        ones = sb("ones", [128, 128])
        adj_sb = sb("adj_sb", [128, N])
        m_qk = sb("m_qk", [128, C, D])
        wv0T = sb("wv0T", [128, C, D])
        w1 = sb("w1", [128, C, D + 2])
        beta = sb("beta", [128, 1])
        nadjT = sb("nadjT", [128, N])
        w2 = sb("w2", [128, C, D])
        rows = sb("rows", [128, 3, D])
        mbias = sb("mbias", [128, N])
        wq3 = sb("wq3", [128, C, D])
        wk3 = sb("wk3", [128, C, D])
        wv3 = sb("wv3", [128, C, D])
        wo3 = sb("wo3", [128, C, D])
        bq = sb("bq", [128, C])
        bk = sb("bk", [128, C])
        mhalf = sb("mhalf", [128, 2])
        stats = sb("stats", [128, 2, 2, 6])
        mv = sb("mv", [128, 2, 2, 2])
        vare = sb("vare", [128, 2, 2])
        nmean = sb("nmean", [128, 2, 2])
        rstd = sb("rstd", [128, 2, 2])
        shift = sb("shift", [128, 2, 2])
        xn = sb("xn", [128, 2, D])
        hT = sb("hT", [128, C, 2, N])
        tT = sb("tT", [128, C, 2, N])
        val = sb("val", [128, 2, D + 2])
        val1 = sb("val1", [128, 2, D + 2])
        relm = sb("relm", [128, 2, N])
        relsq = sb("relsq", [128, 2, N])
        norm2 = sb("norm2", [128, 2])
        rnorm = sb("rnorm", [128, 2])
        wide = [sb(f"wide{g}", [128, HEADS, N]) for g in range(2)]
        prob = [sb(f"prob{g}", [128, HEADS, N]) for g in range(2)]
        probT = sb("probT", [128, HEADS, N])
        qT = sb("qT", [128, C, 2, N])
        kT = sb("kT", [128, C, 2, N])
        small = sb("small", [128, 64])
        oT = sb("oT", [128, 2, C, N])
        adj_pair = adj_sb[:, :].unsqueeze(1).to_broadcast([128, 2, N])
        mbias_pair = mbias[:, :].unsqueeze(1).to_broadcast([128, 2, N])

        def x_of(p, g):
            return xs[:, bass.ds(2 * p + g, 1), :].rearrange("p a d -> p (a d)")

        def x_pair(p):
            return xs[:, bass.ds(2 * p, 2), :]

        def since(n):
            return max(n, 0) if isinstance(n, int) else n

        def layer_norm_stats(dve, p, dve_step, stats_ready, b=0):
            for g in range(2):
                ins = nc.vector.bn_stats(stats[:, b, g, :], x_of(p, g))
            ins.then_inc(dve_step, 1)
            dve.wait_ge(dve_step, 1)
            dve.wait_ge(dve_step, 2 * p + 1)
            for g in range(2):
                ins = nc.vector.bn_aggr(mv[:, b, g, :], stats[:, b, g, :])
            ins.then_inc(dve_step, 1)
            dve.wait_ge(dve_step, 2 * p + 2)
            nc.vector.tensor_scalar(nmean[:, b, :], mv[:, b, :, 0], -1.0, None, ALU.mult)
            nc.vector.tensor_scalar(vare[:, b, :], mv[:, b, :, 1], EPS, None, ALU.add).then_inc(stats_ready, 1)

        def inverse_root(pool, p, stats_ready, rstd_ready, b=0):
            pool.wait_ge(stats_ready, p + 1)
            nc.gpsimd.tensor_tensor(rstd[:, b, :], vare[:, b, :], mhalf[:, :], ALU.pow).then_inc(rstd_ready, 1)

        def root_and_shift(pool, p, stats_ready, rstd_ready, shift_ready, b=0):
            inverse_root(pool, p, stats_ready, rstd_ready, b)
            pool.wait_ge(rstd_ready, p + 1)
            nc.gpsimd.tensor_tensor(shift[:, b, :], nmean[:, b, :], rstd[:, b, :], ALU.mult).then_inc(shift_ready, 1)

        wld = sem("c_weights_loaded")
        c_id0, c_id1, c_ident, c_ones = sem("c_id0"), sem("c_id1"), sem("c_ident"), sem("c_ones")
        c_root, c_mhalf = sem("c_root"), sem("c_mhalf")
        c_pe, c_dve, c_step = sem("c_pe"), sem("c_dve"), sem("c_step")
        with ExitStack() as cctx:
            wq0 = cctx.enter_context(nc.sbuf_tensor("wq0", [128, C, D], F32))
            wk0 = cctx.enter_context(nc.sbuf_tensor("wk0", [128, C, D], F32))
            wv0 = cctx.enter_context(nc.sbuf_tensor("wv0", [128, C, D], F32))
            w1T = cctx.enter_context(nc.sbuf_tensor("w1T", [128, C, D], F32))
            a12 = cctx.enter_context(nc.sbuf_tensor("a12", [128, 2, C], F32))
            row1 = cctx.enter_context(nc.sbuf_tensor("row1", [1, 3 * D + 2], F32))
            deg = cctx.enter_context(nc.sbuf_tensor("deg", [128, 6], F32))
            adjn = cctx.enter_context(nc.sbuf_tensor("adjn", [128, N], F32))

            with nc.Block() as block:
                @block.sync
                def _(sp):
                    w1_cols = w1[:, :, 0:D]
                    for dst, src in ((wq0, w["L0_gnn_Wq"]), (wk0, w["L0_gnn_Wk"]), (wv0, w["L0_gnn_Wv"]),
                                     (w1_cols, w["L1_gnn_W"]), (w2, w["L2_gnn_weight"]), (wq3, w["L3_gnn_Wq"]),
                                     (wk3, w["L3_gnn_Wk"]), (wv3, w["L3_gnn_Wv"]), (wo3, w["L3_gnn_Wo"])):
                        sp.dma_start(dst if dst is w1_cols else dst[:, :, :], src.rearrange("(c p) n -> p c n", p=128)).then_inc(wld, 16)
                    sp.dma_start(adj_sb[:, :], adj).then_inc(wld, 16)
                    with nc.allow_non_contiguous_dma("columns of small vectors"):
                        sp.dma_start(a12[:, :, :].rearrange("p k c -> p (k c)"), w["L1_gnn_a"].rearrange("(k p) o -> p (k o)", p=128)).then_inc(wld, 16)
                        sp.dma_start(bq[:, :], w["L3_gnn_bq"].rearrange("(c p) -> p c", p=128)).then_inc(wld, 16)
                        sp.dma_start(bk[:, :], w["L3_gnn_bk"].rearrange("(c p) -> p c", p=128)).then_inc(wld, 16)
                    for k, name in enumerate(("L2_gnn_bias", "L3_gnn_bv", "L3_gnn_bo")):
                        sp.dma_start(row1[0:1, k * D:(k + 1) * D], w[name].rearrange("(o n) -> o n", o=1)).then_inc(wld, 16)
                    sp.dma_start(row1[0:1, 3 * D:3 * D + 1], w["L1_gnn_beta"].rearrange("(o n) -> o n", o=1)).then_inc(wld, 16)

                LOADED = 16 * 17

                @block.gpsimd
                def _(pool):
                    nc.gpsimd.memset(ones[:, :], 1.0).then_inc(c_ones, 1)
                    nc.gpsimd.memset(mhalf[:, :], -0.5).then_inc(c_mhalf, 1)
                    nc.gpsimd.memset(ident[:, :], 0.0).then_inc(c_id0, 1)
                    pool.wait_ge(c_id0, 1)
                    nc.gpsimd.affine_select(out=ident[:, :], in_=ident[:, :], compare_op=ALU.not_equal, fill=1.0,
                                            base=0, pattern=[[-1, 128]], channel_multiplier=1).then_inc(c_ident, 1)
                    pool.wait_ge(c_mhalf, 1)
                    pool.wait_ge(c_step, 2)
                    nc.gpsimd.tensor_tensor(deg[:, 4:5], deg[:, 2:3], mhalf[:, 0:1], ALU.pow).then_inc(c_root, 1)

                @block.tensor
                def _(pe):
                    pe.wait_ge(wld, LOADED)
                    pe.wait_ge(c_ones, 1)
                    for d in range(C):
                        for e in range(C):
                            ins = nc.tensor.matmul(bank[0][:, d * D:(d + 1) * D], wq0[:, e, d * 128:(d + 1) * 128],
                                                   wk0[:, e, :], start=(e == 0), stop=(e == C - 1))
                    ins.then_inc(c_pe, 1)
                    for k in range(3):
                        ins = nc.tensor.matmul(bank[1 + k // 2][:, (k % 2) * D:(k % 2 + 1) * D], ones[0:1, :],
                                               row1[0:1, k * D:(k + 1) * D], start=True, stop=True)
                    ins = nc.tensor.matmul(bank[2][:, D:D + 1], ones[0:1, :], row1[0:1, 3 * D:3 * D + 1],
                                           start=True, stop=True)
                    ins.then_inc(c_pe, 1)
                    pe.wait_ge(c_ident, 1)
                    for k, src in enumerate((wv0, w1)):
                        for c in range(C):
                            for e in range(C):
                                ins = nc.tensor.transpose(bank[3 + k][:, c * D + e * 128:c * D + (e + 1) * 128],
                                                          src[:, e, c * 128:(c + 1) * 128], ident[:, :])
                    ins.then_inc(c_pe, 1)
                    pe.wait_ge(c_dve, 1)
                    for c in range(C):
                        for f in range(C):
                            ins = nc.tensor.matmul(bank[5][:, 2 * c:2 * c + 2], w1T[:, f, c * 128:(c + 1) * 128],
                                                   a12[:, :, f], start=(f == 0), stop=(f == C - 1))
                    ins.then_inc(c_pe, 1)
                    pe.wait_ge(c_dve, 2)
                    nc.tensor.transpose(bank[6][:, 0:N], adjn[:, :], ident[:, :]).then_inc(c_pe, 1)

                @block.vector
                def _(dve):
                    dve.wait_ge(wld, LOADED)
                    dve.wait_ge(c_pe, 3)
                    nc.vector.tensor_copy(w1T[:, :, :], bank[4][:, :].rearrange("p (c n) -> p c n", c=C)).then_inc(c_dve, 1)
                    nc.vector.tensor_copy(m_qk[:, :, :], bank[0][:, :].rearrange("p (c n) -> p c n", c=C))
                    nc.vector.tensor_copy(wv0T[:, :, :], bank[3][:, :].rearrange("p (c n) -> p c n", c=C))
                    nc.vector.tensor_copy(rows[:, 0:2, :], bank[1][:, :].rearrange("p (c n) -> p c n", c=2))
                    nc.vector.tensor_copy(rows[:, 2, :], bank[2][:, 0:D])
                    nc.vector.tensor_copy(beta[:, :], bank[2][:, D:D + 1])
                    nc.vector.tensor_scalar(mbias[:, :], adj_sb[:, :], -1.0, 1e9, ALU.add, ALU.mult)
                    nc.vector.tensor_scalar(bq[:, :], bq[:, :], QSCALE, None, ALU.mult)
                    nc.vector.tensor_reduce(deg[:, 0:1], adj_sb[:, :], AX_X, ALU.add).then_inc(c_step, 1)
                    dve.wait_ge(c_step, 1)
                    nc.vector.tensor_scalar(deg[:, 1:2], deg[:, 0:1], 0.0, None, ALU.is_gt)
                    nc.vector.tensor_scalar(deg[:, 2:3], deg[:, 0:1], float(np.finfo(np.float32).tiny), None,
                                            ALU.max).then_inc(c_step, 1)
                    dve.wait_ge(c_root, 1)
                    nc.vector.tensor_tensor(deg[:, 3:4], deg[:, 1:2], deg[:, 4:5], ALU.mult).then_inc(c_step, 1)
                    dve.wait_ge(c_step, 3)
                    nc.vector.tensor_scalar(adjn[:, :], adj_sb[:, :], deg[:, 3:4], None, ALU.mult).then_inc(c_dve, 1)
                    dve.wait_ge(c_pe, 5)
                    nc.vector.tensor_copy(w1[:, :, D:D + 2], bank[5][:, 0:2 * C].rearrange("p (c k) -> p c k", c=C))
                    nc.vector.tensor_scalar(nadjT[:, :], bank[6][:, 0:N], deg[:, 3:4], None, ALU.mult).then_inc(c_dve, 1)
                    dve.wait_ge(c_dve, 3)


        def transposes(pe_ps):
            for c in range(C):
                for g in range(2):
                    ins = nc.tensor.transpose(pe_ps[:, c * 2 * N + g * N:c * 2 * N + (g + 1) * N],
                                              xn[:, g, c * 128:(c + 1) * 128], ident[:, :])
            return ins

        def node_product(ps_g, weight, g):
            for c in range(C):
                ins = nc.tensor.matmul(ps_g, hT[:, c, g, :], weight[:, c, :], start=(c == 0), stop=(c == C - 1))
            return ins

        def feature_product(ps, weight):
            for m in range(C):
                for c in range(C):
                    ins = nc.tensor.matmul(ps[:, m * 2 * N:(m + 1) * 2 * N], weight[:, c, m * 128:(m + 1) * 128],
                                           hT[:, c, :, :].rearrange("p g n -> p (g n)"), start=(c == 0), stop=(c == C - 1))
            return ins

        hT_flat = hT[:, :, :, :].rearrange("p c g n -> p (c g n)")

        x_loaded = sem("l0_x_loaded")
        xn_ready, tr_done, hT_ready = sem("l0_xn_ready"), sem("l0_tr_done"), sem("l0_hT_ready")
        t_done, tT_ready, v_done, v_ready = sem("l0_t_done"), sem("l0_tT_ready"), sem("l0_v_done"), sem("l0_v_ready")
        rel_done, relm_ready, relsq_ready = sem("l0_rel_done"), sem("l0_relm_ready"), sem("l0_relsq_ready")
        n2_ready, rn_ready = sem("l0_norm2_ready"), sem("l0_rnorm_ready")
        stats_ready, rstd_ready = sem("l0_stats_ready"), sem("l0_rstd_ready")
        out_done, x_done, dstep = sem("l0_out_done"), sem("l0_x_done"), sem("l0_dve_step")
        HT, TT, VV, RR, NO, OO = bank[0:6]

        with nc.Block() as block:
            @block.sync
            def _(sp):
                sp.dma_start(xs[:, 0:2, :], x[0:2, :, :].rearrange("g n d -> n g d")).then_inc(x_loaded, 16)
                with sp.Fori(1, PAIRS) as p:
                    sp.wait_ge(x_loaded, 16 * p)
                    sp.dma_start(x_pair(p), x[bass.ds(2 * p, 2), :, :].rearrange("g n d -> n g d")).then_inc(x_loaded, 16)

            @block.tensor
            def _(pe):
                def turn(p):
                    pe.wait_ge(xn_ready, p + 1)
                    transposes(HT).then_inc(tr_done, 1)

                def t_product(p):
                    pe.wait_ge(hT_ready, p + 1)
                    feature_product(TT, m_qk).then_inc(t_done, 1)

                def values(p):
                    pe.wait_ge(v_ready, since(p))
                    for g in range(2):
                        ins = node_product(VV[:, g * D:(g + 1) * D], wv0T, g)
                    ins.then_inc(v_done, 1)

                def relation(p):
                    pe.wait_ge(tT_ready, p + 1)
                    pe.wait_ge(relm_ready, since(p))
                    for g in range(2):
                        for c in range(C):
                            ins = nc.tensor.matmul(RR[:, g * N:(g + 1) * N], hT[:, c, g, :], tT[:, c, g, :],
                                                   start=(c == 0), stop=(c == C - 1))
                    ins.then_inc(rel_done, 1)

                def outputs(p):
                    pe.wait_ge(relsq_ready, p + 1)
                    pe.wait_ge(x_done, since(p))
                    for g in range(2):
                        nc.tensor.matmul(NO[:, g:g + 1], relsq[:, g, :], ones[:, 0:1], start=True, stop=True)
                    pe.wait_ge(v_ready, p + 1)
                    for g in range(2):
                        ins = nc.tensor.matmul(OO[:, g * D:(g + 1) * D], relm[:, g, :], val[:, g, 0:D], start=True, stop=True)
                    ins.then_inc(out_done, 1)

                turn(0)
                t_product(0)
                turn(1)
                values(0)
                relation(0)

                def step(p):
                    t_product(p)
                    turn(p + 1)
                    values(p)
                    relation(p)
                    outputs(p - 1)

                step(1)
                with pe.Fori(2, PAIRS - 1) as p:
                    step(p)
                t_product(PAIRS - 1)
                values(PAIRS - 1)
                relation(PAIRS - 1)
                outputs(PAIRS - 2)
                outputs(PAIRS - 1)

            @block.scalar
            def _(act):
                def relu_T(p):
                    act.wait_ge(tr_done, p + 1)
                    act.wait_ge(rel_done, since(p))
                    nc.scalar.activation(hT_flat, HT[:, :], ACT.Relu).then_inc(hT_ready, 1)

                def copy_t(p):
                    act.wait_ge(t_done, p + 1)
                    nc.scalar.copy(tT[:, :, :, :].rearrange("p c g n -> p (c g n)"), TT[:, :]).then_inc(tT_ready, 1)

                def copy_v(p):
                    act.wait_ge(v_done, p + 1)
                    act.wait_ge(out_done, since(p))
                    nc.scalar.copy(val[:, :, 0:D], VV[:, :].rearrange("p (g n) -> p g n", g=2)).then_inc(v_ready, 1)

                relu_T(0)
                copy_t(0)
                copy_v(0)
                relu_T(1)
                with act.Fori(1, PAIRS - 1) as p:
                    copy_t(p)
                    relu_T(p + 1)
                    copy_v(p)
                copy_t(PAIRS - 1)
                copy_v(PAIRS - 1)

            @block.gpsimd
            def _(pool):
                def squares(p):
                    pool.wait_ge(relm_ready, p + 1)
                    nc.gpsimd.tensor_tensor(relsq[:, :, :], relm[:, :, :], relm[:, :, :], ALU.mult).then_inc(relsq_ready, 1)

                def inverse_norm(p):
                    pool.wait_ge(n2_ready, p + 1)
                    nc.gpsimd.tensor_tensor(rnorm[:, :], norm2[:, :], mhalf[:, :], ALU.pow).then_inc(rn_ready, 1)

                for p in range(3):
                    inverse_root(pool, p, stats_ready, rstd_ready)
                squares(0)
                with pool.Fori(1, PAIRS - 2) as p:
                    inverse_root(pool, p + 2, stats_ready, rstd_ready)
                    squares(p)
                    inverse_norm(p - 1)
                for p in range(PAIRS - 2, PAIRS):
                    squares(p)
                    inverse_norm(p - 1)
                inverse_norm(PAIRS - 1)

            @block.vector
            def _(dve):
                def statistics(p):
                    dve.wait_ge(x_loaded, 16 * p + 16)
                    layer_norm_stats(dve, p, dstep, stats_ready)

                def normalise(p):
                    dve.wait_ge(rstd_ready, p + 1)
                    dve.wait_ge(tr_done, since(p))
                    for g in range(2):
                        ins = nc.vector.tensor_scalar(xn[:, g, :], x_of(p, g), mv[:, 0, g, 0:1], rstd[:, 0, g:g + 1],
                                                      ALU.subtract, ALU.mult)
                    ins.then_inc(xn_ready, 1)

                def mask(p):
                    dve.wait_ge(rel_done, p + 1)
                    dve.wait_ge(out_done, since(p))
                    nc.vector.tensor_tensor(relm[:, :, :], RR[:, 0:2 * N].rearrange("p (g n) -> p g n", g=2),
                                            adj_pair, ALU.mult).then_inc(relm_ready, 1)

                def copy_norm2(p):
                    dve.wait_ge(out_done, p + 1)
                    nc.vector.tensor_copy(norm2[:, :], NO[:, 0:2]).then_inc(n2_ready, 1)

                def update(p):
                    dve.wait_ge(rn_ready, p + 1)
                    for g in range(2):
                        ins = nc.vector.scalar_tensor_tensor(x_of(p, g), OO[:, g * D:(g + 1) * D], rnorm[:, g:g + 1],
                                                             x_of(p, g), ALU.mult, ALU.add)
                    ins.then_inc(x_done, 1)

                for p in range(3):
                    statistics(p)
                    normalise(p)
                mask(0)
                with dve.Fori(1, PAIRS - 2) as p:
                    statistics(p + 2)
                    mask(p)
                    copy_norm2(p - 1)
                    normalise(p + 2)
                    update(p - 1)
                for p in range(PAIRS - 2, PAIRS):
                    mask(p)
                    copy_norm2(p - 1)
                    update(p - 1)
                copy_norm2(PAIRS - 1)
                update(PAIRS - 1)
                dve.wait_ge(x_done, PAIRS)

        xn_ready, tr_done, hT_ready = sem("l1_xn_ready"), sem("l1_tr_done"), sem("l1_hT_ready")
        h_done, val_ready, diag_ready, e_done = sem("l1_h_done"), sem("l1_val_ready"), sem("l1_diag_ready"), sem("l1_e_done")
        e_ready, em_ready, max_ready, nmax_ready = sem("l1_e_ready"), sem("l1_em_ready"), sem("l1_max_ready"), sem("l1_nmax_ready")
        prob_ready, pt_done, pt_ready, att_done = sem("l1_prob_ready"), sem("l1_pt_done"), sem("l1_pt_ready"), sem("l1_att_done")
        rinv_ready, bh_ready, u_ready, umin_ready = sem("l1_rinv_ready"), sem("l1_bh_ready"), sem("l1_u_ready"), sem("l1_umin_ready")
        eu_ready, elu_ready, x_done, dstep = sem("l1_eu_ready"), sem("l1_elu_ready"), sem("l1_x_done"), sem("l1_dve_step")
        leaky_ready = sem("l1_leaky_ready")
        stats_ready, rstd_ready, shift_ready = sem("l1_stats_ready"), sem("l1_rstd_ready"), sem("l1_shift_ready")
        HT, HG, PT, EE, UU = bank[0], (bank[1], bank[2]), bank[3], bank[4], bank[5]
        valb = [val, val1]
        bh = [wide[b][:, 0:4, :].rearrange("p a n -> p (a n)").rearrange("p (g d) -> p g d", g=2) for b in range(2)]
        u_sb = wide[0][:, 4:8, :].rearrange("p a n -> p (a n)")
        umin = wide[1][:, 4:8, :].rearrange("p a n -> p (a n)")
        eu = prob[0][:, 0:4, :].rearrange("p a n -> p (a n)")
        elu = prob[0][:, 4:8, :].rearrange("p a n -> p (a n)")
        e_sb, em, p1, p1T = (prob[1][:, 2 * k:2 * k + 2, :] for k in range(4))
        diag, el = tT[:, 0, :, :], tT[:, 1, :, :]
        nmax, rsum, rinv = small[:, 0:2], small[:, 2:4], small[:, 4:6]
        mx = small[:, 8:10]

        with nc.Block() as block:
            @block.tensor
            def _(pe):
                def turn(p):
                    pe.wait_ge(xn_ready, p + 1)
                    transposes(HT).then_inc(tr_done, 1)

                def product(p):
                    pe.wait_ge(hT_ready, p + 1)
                    pe.wait_ge(val_ready, since(p))
                    for g in range(2):
                        ins = node_product(HG[g][:, 0:D + 2], w1, g)
                    ins.then_inc(h_done, 1)

                def turn_prob(p):
                    pe.wait_ge(prob_ready, p + 1)
                    pe.wait_ge(pt_ready, since(p))
                    for g in range(2):
                        ins = nc.tensor.transpose(PT[:, g * N:(g + 1) * N], p1[:, g, :], ident[:, :])
                    ins.then_inc(pt_done, 1)

                def spread(p):
                    pe.wait_ge(diag_ready, p + 1)
                    pe.wait_ge(e_ready, since(p))
                    nc.tensor.matmul(EE[:, 0:2 * N], ones[:, :], diag.rearrange("p g n -> p (g n)"),
                                     start=True, stop=True).then_inc(e_done, 1)

                def attend(p, b):
                    pe.wait_ge(pt_ready, p + 1)
                    pe.wait_ge(u_ready, since(p))
                    for g in range(2):
                        ins = nc.tensor.matmul(UU[:, g * D:(g + 1) * D], p1T[:, g, :], valb[b][:, g, 0:D], start=True, stop=True)
                    ins.then_inc(att_done, 1)

                def step(p, b, first=False, last=False):
                    product(p)
                    if not last:
                        turn(p + 1)
                    if not first:
                        turn_prob(p - 1)
                    spread(p)
                    if not first:
                        attend(p - 1, 1 - b)

                turn(0)
                step(0, 0, first=True)
                step(1, 1)
                with pe.Fori(1, PAIRS // 2 - 1) as j:
                    for b in range(2):
                        step(2 * j + b, b)
                step(PAIRS - 2, 0)
                step(PAIRS - 1, 1, last=True)
                turn_prob(PAIRS - 1)
                attend(PAIRS - 1, 1)

            @block.scalar
            def _(act):
                def normalise(p, b):
                    act.wait_ge(shift_ready, p + 1)
                    act.wait_ge(tr_done, since(p))
                    for g in range(2):
                        ins = nc.scalar.activation(xn[:, g, :], x_of(p, g), ACT.Relu, bias=shift[:, b, g:g + 1],
                                                   scale=rstd[:, b, g:g + 1])
                    ins.then_inc(xn_ready, 1)

                def copy_hT(p):
                    act.wait_ge(tr_done, p + 1)
                    act.wait_ge(h_done, since(p))
                    nc.scalar.copy(hT_flat, HT[:, :]).then_inc(hT_ready, 1)

                def copy_h(p, b):
                    act.wait_ge(h_done, p + 1)
                    act.wait_ge(att_done, since(p - 1))
                    act.wait_ge(bh_ready, since(p - 1))
                    for g in range(2):
                        ins = nc.scalar.copy(valb[b][:, g, :], HG[g][:, 0:D + 2])
                    ins.then_inc(val_ready, 1)

                def add_s1(p, b):
                    act.wait_ge(e_done, p + 1)
                    act.wait_ge(leaky_ready, since(p))
                    for g in range(2):
                        ins = nc.scalar.activation(e_sb[:, g, :], EE[:, g * N:(g + 1) * N], ACT.Identity,
                                                   bias=valb[b][:, g, D:D + 1])
                    ins.then_inc(e_ready, 1)

                def softmax_exp(p):
                    act.wait_ge(nmax_ready, p + 1)
                    act.wait_ge(pt_done, since(p))
                    act.wait_ge(rinv_ready, since(p))
                    for g in range(2):
                        ins = nc.scalar.activation(p1[:, g, :], em[:, g, :], ACT.Exp, bias=nmax[:, g:g + 1],
                                                   accum_out=rsum[:, g:g + 1])
                    ins.then_inc(prob_ready, 1)

                def elu_exp(p):
                    act.wait_ge(umin_ready, p + 1)
                    act.wait_ge(elu_ready, since(p))
                    nc.scalar.activation(eu, umin, ACT.Exp).then_inc(eu_ready, 1)

                def step(p, b, first=False, last=False):
                    copy_h(p, b)
                    if not last:
                        copy_hT(p + 1)
                    add_s1(p, b)
                    if not last:
                        if isinstance(p, int) and p + 2 >= PAIRS:
                            pass
                        else:
                            normalise(p + 2, b)
                    softmax_exp(p)
                    if not first:
                        elu_exp(p - 1)

                normalise(0, 0)
                copy_hT(0)
                normalise(1, 1)
                step(0, 0, first=True)
                step(1, 1)
                with act.Fori(1, PAIRS // 2 - 1) as j:
                    for b in range(2):
                        step(2 * j + b, b)
                step(PAIRS - 2, 0)
                step(PAIRS - 1, 1, last=True)
                elu_exp(PAIRS - 1)

            @block.gpsimd
            def _(pool):
                def diagonal(p, b):
                    pool.wait_ge(val_ready, p + 1)
                    pool.wait_ge(e_done, since(p))
                    for g in range(2):
                        ins = nc.gpsimd.tensor_tensor(diag[:, g, :], ident[:, :], valb[b][:, g, D + 1:D + 2].to_broadcast([128, N]), ALU.mult)
                    ins.then_inc(diag_ready, 1)

                def beta_h(p, b):
                    pool.wait_ge(u_ready, since(p - 1))
                    nc.gpsimd.tensor_tensor(bh[b], valb[b][:, :, 0:D], beta[:, :].unsqueeze(2).to_broadcast([128, 2, D]), ALU.mult).then_inc(bh_ready, 1)

                def add(p):
                    pool.wait_ge(elu_ready, p + 1)
                    nc.gpsimd.tensor_tensor(x_pair(p), x_pair(p), elu.rearrange("p (g d) -> p g d", g=2),
                                            ALU.add).then_inc(x_done, 1)

                def step(p, b, lag=2, norms=True):
                    diagonal(p, b)
                    beta_h(p, b)
                    if norms:
                        root_and_shift(pool, p + 3, stats_ready, rstd_ready, shift_ready, 1 - b)
                    if lag >= 2:
                        add(p - 2)

                for p in range(3):
                    root_and_shift(pool, p, stats_ready, rstd_ready, shift_ready, p % 2)
                step(0, 0, lag=0)
                step(1, 1, lag=1)
                with pool.Fori(1, PAIRS // 2 - 2) as j:
                    for b in range(2):
                        step(2 * j + b, b)
                for p in range(PAIRS - 4, PAIRS):
                    step(p, p % 2, norms=p + 3 < PAIRS)
                add(PAIRS - 2)
                add(PAIRS - 1)

            @block.vector
            def _(dve):
                def norm(p, b):
                    dve.wait_ge(xn_ready, since(p - 1))
                    layer_norm_stats(dve, p, dstep, stats_ready, b)

                def copy_pT(p):
                    dve.wait_ge(pt_done, p + 1)
                    dve.wait_ge(att_done, since(p))
                    nc.vector.tensor_copy(p1T, PT[:, 0:2 * N].rearrange("p (g n) -> p g n", g=2)).then_inc(pt_ready, 1)
                    nc.vector.reciprocal(rinv, rsum).then_inc(rinv_ready, 1)

                def elu_max(p):
                    dve.wait_ge(eu_ready, p + 1)
                    dve.wait_ge(x_done, since(p))
                    nc.vector.scalar_tensor_tensor(elu, eu, -1.0, u_sb, ALU.add, ALU.max).then_inc(elu_ready, 1)

                def mask_max(p):
                    dve.wait_ge(e_ready, p + 1)
                    nc.vector.scalar_tensor_tensor(el, e_sb, ALPHA, e_sb, ALU.mult, ALU.max).then_inc(leaky_ready, 1)
                    dve.wait_ge(leaky_ready, p + 1)
                    dve.wait_ge(prob_ready, since(p))
                    nc.vector.tensor_tensor(em, el, adj_pair, ALU.mult).then_inc(em_ready, 1)
                    dve.wait_ge(em_ready, p + 1)
                    nc.vector.tensor_reduce(mx, em, AX_X, ALU.max).then_inc(max_ready, 1)
                    dve.wait_ge(max_ready, p + 1)
                    nc.vector.tensor_scalar(nmax, mx, -1.0, None, ALU.mult).then_inc(nmax_ready, 1)

                def gather(p, b):
                    dve.wait_ge(att_done, p + 1)
                    dve.wait_ge(bh_ready, p + 1)
                    dve.wait_ge(rinv_ready, p + 1)
                    dve.wait_ge(elu_ready, since(p))
                    for g in range(2):
                        ins = nc.vector.scalar_tensor_tensor(u_sb[:, g * D:(g + 1) * D], UU[:, g * D:(g + 1) * D],
                                                             rinv[:, g:g + 1], bh[b][:, g, :], ALU.mult, ALU.add)
                    ins.then_inc(u_ready, 1)
                    dve.wait_ge(u_ready, p + 1)
                    dve.wait_ge(eu_ready, since(p))
                    nc.vector.tensor_scalar(umin, u_sb, 0.0, None, ALU.min).then_inc(umin_ready, 1)

                def step(p, b, lag=2, norms=True):
                    if lag >= 1:
                        copy_pT(p - 1)
                    if lag >= 2:
                        elu_max(p - 2)
                    mask_max(p)
                    if norms:
                        norm(p + 3, 1 - b)
                    if lag >= 1:
                        gather(p - 1, 1 - b)

                norm(0, 0)
                norm(1, 1)
                norm(2, 0)
                step(0, 0, lag=0)
                step(1, 1, lag=1)
                step(2, 0)
                step(3, 1)
                with dve.Fori(2, PAIRS // 2 - 2) as j:
                    for b in range(2):
                        step(2 * j + b, b)
                for p in range(PAIRS - 4, PAIRS):
                    step(p, p % 2, norms=p + 3 < PAIRS)
                copy_pT(PAIRS - 1)
                elu_max(PAIRS - 2)
                gather(PAIRS - 1, 1)
                elu_max(PAIRS - 1)

        xn_ready, yt_done, yt_ready, out_done = sem("l2_xn_ready"), sem("l2_yt_done"), sem("l2_yt_ready"), sem("l2_out_done")
        bias_done, x_done, dstep = sem("l2_bias_done"), sem("l2_x_done"), sem("l2_dve_step")
        stats_ready, rstd_ready, shift_ready = sem("l2_stats_ready"), sem("l2_rstd_ready"), sem("l2_shift_ready")
        YT, OO = bank[0:2], bank[2:4]
        yT = [tT, hT]

        with nc.Block() as block:
            @block.tensor
            def _(pe):
                def gather(p, b):
                    pe.wait_ge(xn_ready, p + 1)
                    pe.wait_ge(yt_ready, since(p - 1))
                    for c in range(C):
                        for g in range(2):
                            ins = nc.tensor.matmul(YT[b][:, (2 * c + g) * N:(2 * c + g + 1) * N],
                                                   xn[:, g, c * 128:(c + 1) * 128], nadjT[:, :], start=True, stop=True)
                    ins.then_inc(yt_done, 1)

                def outputs(p, b):
                    pe.wait_ge(yt_ready, p + 1)
                    pe.wait_ge(x_done, since(p - 1))
                    for g in range(2):
                        for c in range(C):
                            ins = nc.tensor.matmul(OO[b][:, g * D:(g + 1) * D], yT[b][:, c, g, :], w2[:, c, :],
                                                   start=(c == 0), stop=(c == C - 1))
                    ins.then_inc(out_done, 1)

                gather(0, 0)
                gather(1, 1)
                outputs(0, 0)
                for p in range(2, 4):
                    gather(p, p % 2)
                    outputs(p - 1, (p - 1) % 2)
                with pe.Fori(2, PAIRS // 2) as j:
                    for b in range(2):
                        gather(2 * j + b, b)
                        outputs(2 * j + b - 1, 1 - b)
                outputs(PAIRS - 1, 1)

            @block.scalar
            def _(act):
                def normalise(p, b):
                    act.wait_ge(shift_ready, p + 1)
                    act.wait_ge(yt_done, since(p))
                    for g in range(2):
                        ins = nc.scalar.activation(xn[:, g, :], x_of(p, g), ACT.Relu, bias=shift[:, b, g:g + 1],
                                                   scale=rstd[:, b, g:g + 1])
                    ins.then_inc(xn_ready, 1)

                def copy_yT(p, b):
                    act.wait_ge(yt_done, p + 1)
                    act.wait_ge(out_done, since(p - 1))
                    nc.scalar.copy(yT[b][:, :, :, :].rearrange("p c g n -> p (c g n)"), YT[b][:, :]).then_inc(yt_ready, 1)

                normalise(0, 0)
                normalise(1, 1)
                copy_yT(0, 0)
                for p in range(2, 4):
                    normalise(p, p % 2)
                    copy_yT(p - 1, (p - 1) % 2)
                with act.Fori(2, PAIRS // 2) as j:
                    for b in range(2):
                        normalise(2 * j + b, b)
                        copy_yT(2 * j + b - 1, 1 - b)
                copy_yT(PAIRS - 1, 1)

            @block.gpsimd
            def _(pool):
                def add_bias(p):
                    pool.wait_ge(xn_ready, p + 1)
                    nc.gpsimd.tensor_tensor(x_pair(p), x_pair(p), rows[:, 0:1, :].to_broadcast([128, 2, D]),
                                            ALU.add).then_inc(bias_done, 1)

                root_and_shift(pool, 0, stats_ready, rstd_ready, shift_ready, 0)
                root_and_shift(pool, 1, stats_ready, rstd_ready, shift_ready, 1)
                with pool.Fori(1, PAIRS // 2) as j:
                    for b in range(2):
                        root_and_shift(pool, 2 * j + b, stats_ready, rstd_ready, shift_ready, b)
                        add_bias(2 * j + b - 2)
                add_bias(PAIRS - 2)
                add_bias(PAIRS - 1)

            @block.vector
            def _(dve):
                def norm(p, b):
                    dve.wait_ge(xn_ready, since(p - 1))
                    layer_norm_stats(dve, p, dstep, stats_ready, b)

                def update(p, b):
                    dve.wait_ge(out_done, p + 1)
                    dve.wait_ge(bias_done, p + 1)
                    nc.vector.tensor_tensor(x_pair(p), OO[b][:, :].rearrange("p (g d) -> p g d", g=2), x_pair(p),
                                            ALU.add).then_inc(x_done, 1)

                norm(0, 0)
                norm(1, 1)
                with dve.Fori(1, PAIRS // 2) as j:
                    for b in range(2):
                        norm(2 * j + b, b)
                        update(2 * j + b - 2, b)
                update(PAIRS - 2, 0)
                update(PAIRS - 1, 1)

        xn_ready, tr_done, hT_ready = sem("l3_xn_ready"), sem("l3_tr_done"), sem("l3_hT_ready")
        q_done, q_ready, k_done, k_ready = sem("l3_q_done"), sem("l3_q_ready"), sem("l3_k_done"), sem("l3_k_ready")
        v_done, v_ready, s_done, s_masked = sem("l3_v_done"), sem("l3_v_ready"), sem("l3_s_done"), sem("l3_s_masked")
        max_ready, nmax_ready, exp_done, rinv_ready = sem("l3_max_ready"), sem("l3_nmax_ready"), sem("l3_exp_done"), sem("l3_rinv_ready")
        prob_ready, pt_done, pt_ready = sem("l3_prob_ready"), sem("l3_pt_done"), sem("l3_pt_ready")
        o_done, o_ready, y_done, x_done = sem("l3_o_done"), sem("l3_o_ready"), sem("l3_y_done"), sem("l3_x_done")
        stats_ready, rstd_ready = sem("l3_stats_ready"), sem("l3_rstd_ready")
        bias_done, dstep, stored = sem("l3_bias_done"), sem("l3_dve_step"), sem("l3_stored")
        SS, PT, MA, MB = bank[0:4], bank[4:6], bank[6], bank[7]
        nmax = [small[:, 8 * g:8 * g + 8] for g in range(2)]
        mx = small[:, 16:24]
        rsum = [small[:, 24 + 8 * g:32 + 8 * g] for g in range(2)]
        rinv = [small[:, 40 + 8 * g:48 + 8 * g] for g in range(2)]

        with nc.Block() as block:
            @block.tensor
            def _(pe):
                def turn(p):
                    pe.wait_ge(xn_ready, p + 1)
                    pe.wait_ge(o_ready, since(2 * p - 2))
                    transposes(MA).then_inc(tr_done, 1)

                def project_qk(p):
                    pe.wait_ge(hT_ready, p + 1)
                    feature_product(MA, wq3).then_inc(q_done, 1)
                    pe.wait_ge(x_done, since(p - 1))
                    feature_product(MB, wk3).then_inc(k_done, 1)

                def project_v(t, g):
                    node_product(MB[:, 0:D], wv3, g).then_inc(v_done, 1)

                def scores(t, g):
                    for r in range(R):
                        pe.wait_ge(s_masked, since(R * t + r + 1 - R))
                        for c in range(C):
                            rows_r = slice(HD * r, HD * (r + 1))
                            ins = nc.tensor.matmul(SS[r][:, c * N:(c + 1) * N], qT[rows_r, c, g, :], kT[rows_r, c, g, :],
                                                   start=True, stop=True)
                        ins.then_inc(s_done, 1)

                def attend(t, g):
                    pe.wait_ge(prob_ready, t + 1)
                    for c in range(C):
                        pe.wait_ge(pt_ready, since(2 * t + c - 1))
                        for r in range(R):
                            ins = nc.tensor.transpose(PT[c][:, r * N:(r + 1) * N], prob[g][:, r * C + c, :], ident[:, :])
                        ins.then_inc(pt_done, 1)
                    pe.wait_ge(v_ready, t + 1)
                    for c in range(C):
                        pe.wait_ge(pt_ready, 2 * t + c + 1)
                        for r in range(R):
                            h = c * R + r
                            ins = nc.tensor.matmul(MA[HD * r:HD * (r + 1), c * N:(c + 1) * N],
                                                   val[:, g, HD * h:HD * (h + 1)], probT[:, h, :], start=True, stop=True)
                    ins.then_inc(o_done, 1)

                def project_o(p):
                    pe.wait_ge(o_ready, 2 * p + 2)
                    for g in range(2):
                        for c in range(C):
                            ins = nc.tensor.matmul(MB[:, g * D:(g + 1) * D], oT[:, g, c, :], wo3[:, c, :],
                                                   start=(c == 0), stop=(c == C - 1))
                    ins.then_inc(y_done, 1)

                def pair(p, first=False, last=False):
                    pe.wait_ge(q_ready, p + 1)
                    pe.wait_ge(k_ready, p + 1)
                    scores(2 * p, 0)
                    if not first:
                        pe.wait_ge(o_ready, 2 * p - 1)
                        attend(2 * p - 1, 1)
                    pe.wait_ge(v_ready, 2 * p + 1)
                    project_v(2 * p + 1, 1)
                    if not last:
                        turn(p + 1)
                    if not first:
                        pe.wait_ge(v_ready, 2 * p + 2)
                        project_o(p - 1)
                    scores(2 * p + 1, 1)
                    if not last:
                        if first:
                            pe.wait_ge(v_ready, 2)
                        project_qk(p + 1)
                        pe.wait_ge(q_ready, p + 2)
                    attend(2 * p, 0)
                    if not last:
                        pe.wait_ge(k_ready, p + 2)
                        project_v(2 * p + 2, 0)

                turn(0)
                project_qk(0)
                pe.wait_ge(k_ready, 1)
                project_v(0, 0)
                pair(0, first=True)
                with pe.Fori(1, PAIRS - 1) as p:
                    pair(p)
                pair(PAIRS - 1, last=True)
                pe.wait_ge(o_ready, 2 * PAIRS - 1)
                attend(2 * PAIRS - 1, 1)
                project_o(PAIRS - 1)

            @block.scalar
            def _(act):
                def relu_T(p):
                    act.wait_ge(tr_done, p + 1)
                    nc.scalar.activation(hT_flat, MA[:, :], ACT.Relu).then_inc(hT_ready, 1)

                def copy_q(p):
                    act.wait_ge(q_done, p + 1)
                    for c in range(C):
                        ins = nc.scalar.activation(qT[:, c, :, :].rearrange("p g n -> p (g n)"), MA[:, c * 2 * N:(c + 1) * 2 * N],
                                                   ACT.Identity, bias=bq[:, c:c + 1], scale=QSCALE)
                    ins.then_inc(q_ready, 1)

                def exponentials(t, g, half):
                    if half == 0:
                        act.wait_ge(nmax_ready, t + 1)
                    for k in range(4 * half, 4 * half + 4):
                        ins = nc.scalar.activation(prob[g][:, k, :], wide[g][:, k, :], ACT.Exp, bias=nmax[g][:, k:k + 1],
                                                   accum_out=rsum[g][:, k:k + 1])
                    if half == 1:
                        ins.then_inc(exp_done, 1)

                def copy_pT(t):
                    for c in range(C):
                        act.wait_ge(pt_done, 2 * t + c + 1)
                        if c == 0:
                            act.wait_ge(o_done, since(t))
                        nc.scalar.copy(probT[:, c * R:(c + 1) * R, :].rearrange("p r n -> p (r n)"),
                                       PT[c][:, :]).then_inc(pt_ready, 1)

                def copy_o(t, g):
                    act.wait_ge(o_done, t + 1)
                    nc.scalar.copy(oT[:, g, :, :].rearrange("p c n -> p (c n)"), MA[:, 0:D]).then_inc(o_ready, 1)

                def pair(p, first=False, last=False):
                    if not first:
                        copy_pT(2 * p - 1)
                    exponentials(2 * p, 0, 0)
                    if not first:
                        copy_o(2 * p - 1, 1)
                    exponentials(2 * p, 0, 1)
                    if not last:
                        relu_T(p + 1)
                        copy_q(p + 1)
                    exponentials(2 * p + 1, 1, 0)
                    copy_pT(2 * p)
                    exponentials(2 * p + 1, 1, 1)
                    copy_o(2 * p, 0)

                relu_T(0)
                copy_q(0)
                pair(0, first=True)
                with act.Fori(1, PAIRS - 1) as p:
                    pair(p)
                pair(PAIRS - 1, last=True)
                copy_pT(2 * PAIRS - 1)
                copy_o(2 * PAIRS - 1, 1)

            @block.gpsimd
            def _(pool):
                def add_bias(p):
                    pool.wait_ge(xn_ready, p + 1)
                    nc.gpsimd.tensor_tensor(x_pair(p), x_pair(p), rows[:, 2:3, :].to_broadcast([128, 2, D]),
                                            ALU.add).then_inc(bias_done, 1)

                def divide(t, g):
                    pool.wait_ge(rinv_ready, t + 1)
                    nc.gpsimd.tensor_tensor(prob[g][:, :, :], prob[g][:, :, :],
                                            rinv[g].unsqueeze(2).to_broadcast([128, HEADS, N]),
                                            ALU.mult).then_inc(prob_ready, 1)

                def pair(p, norms=True):
                    add_bias(p)
                    divide(2 * p, 0)
                    if norms:
                        inverse_root(pool, p + 2, stats_ready, rstd_ready)
                    divide(2 * p + 1, 1)

                inverse_root(pool, 0, stats_ready, rstd_ready)
                inverse_root(pool, 1, stats_ready, rstd_ready)
                with pool.Fori(0, PAIRS - 2) as p:
                    pair(p)
                pair(PAIRS - 2, norms=False)
                pair(PAIRS - 1, norms=False)

            @block.vector
            def _(dve):
                def normalise(p):
                    dve.wait_ge(rstd_ready, p + 1)
                    dve.wait_ge(tr_done, since(p))
                    for g in range(2):
                        ins = nc.vector.tensor_scalar(xn[:, g, :], x_of(p, g), mv[:, 0, g, 0:1], rstd[:, 0, g:g + 1],
                                                      ALU.subtract, ALU.mult)
                    ins.then_inc(xn_ready, 1)

                def copy_k(p):
                    dve.wait_ge(k_done, p + 1)
                    for c in range(C):
                        ins = nc.vector.tensor_scalar(kT[:, c, :, :].rearrange("p g n -> p (g n)"), MB[:, c * 2 * N:(c + 1) * 2 * N],
                                                      bk[:, c:c + 1], None, ALU.add)
                    ins.then_inc(k_ready, 1)

                def copy_v(t, g):
                    dve.wait_ge(v_done, t + 1)
                    nc.vector.tensor_tensor(val[:, g, 0:D], MB[:, 0:D], rows[:, 1, :], ALU.add).then_inc(v_ready, 1)

                def mask_max(t, g):
                    for r in range(R):
                        dve.wait_ge(s_done, R * t + r + 1)
                        nc.vector.tensor_tensor(wide[g][:, r * C:(r + 1) * C, :],
                                                SS[r][:, 0:C * N].rearrange("p (c n) -> p c n", c=C),
                                                mbias_pair, ALU.add).then_inc(s_masked, 1)
                    dve.wait_ge(s_masked, R * t + R)
                    nc.vector.tensor_reduce(mx, wide[g][:, :, :], AX_X, ALU.max).then_inc(max_ready, 1)
                    dve.wait_ge(max_ready, t + 1)
                    nc.vector.tensor_scalar(nmax[g], mx, -1.0, None, ALU.mult).then_inc(nmax_ready, 1)

                def inverse(t, g):
                    dve.wait_ge(exp_done, t + 1)
                    nc.vector.reciprocal(rinv[g], rsum[g]).then_inc(rinv_ready, 1)

                def update(p):
                    dve.wait_ge(y_done, p + 1)
                    dve.wait_ge(bias_done, p + 1)
                    nc.vector.tensor_tensor(x_pair(p), MB[:, :].rearrange("p (g d) -> p g d", g=2), x_pair(p),
                                            ALU.add).then_inc(x_done, 1)

                def pair(p, first=False, last=False, norms=True):
                    mask_max(2 * p, 0)
                    copy_v(2 * p + 1, 1)
                    inverse(2 * p, 0)
                    if not first:
                        update(p - 1)
                    mask_max(2 * p + 1, 1)
                    if norms:
                        layer_norm_stats(dve, p + 2, dstep, stats_ready)
                    if not last:
                        copy_k(p + 1)
                    if norms:
                        normalise(p + 2)
                    inverse(2 * p + 1, 1)
                    if not last:
                        copy_v(2 * p + 2, 0)

                for p in range(2):
                    layer_norm_stats(dve, p, dstep, stats_ready)
                    normalise(p)
                copy_k(0)
                copy_v(0, 0)
                pair(0, first=True)
                with dve.Fori(1, PAIRS - 2) as p:
                    pair(p)
                pair(PAIRS - 2, norms=False)
                pair(PAIRS - 1, last=True, norms=False)
                update(PAIRS - 1)

            @block.sync
            def _(sp):
                with sp.Fori(0, PAIRS) as p:
                    sp.wait_ge(x_done, 1)
                    sp.wait_ge(x_done, p + 1)
                    sp.dma_start(out[bass.ds(2 * p, 2), :, :].rearrange("g n d -> n g d"), x_pair(p)).then_inc(stored, 16)
                sp.wait_ge(stored, 16 * PAIRS)


_INS = ["x", "adj", "L0_gnn_Wq", "L0_gnn_Wk", "L0_gnn_Wv", "L1_gnn_W", "L1_gnn_a", "L1_gnn_beta", "L2_gnn_weight",
        "L2_gnn_bias", "L3_gnn_Wq", "L3_gnn_bq", "L3_gnn_Wk", "L3_gnn_bk", "L3_gnn_Wv", "L3_gnn_bv", "L3_gnn_Wo", "L3_gnn_bo"]


def kernel(**inputs):
    import numpy as _np
    import concourse.bacc as _bacc
    from concourse import mybir as _mybir
    from concourse.bass_utils import run_bass_kernel_spmd as _run

    nc = _bacc.Bacc("TRN2", target_bir_lowering=False, num_devices=1)
    arrays, aps = {}, {}
    for name in _INS:
        a = _np.ascontiguousarray(inputs[name])
        arrays[f"in_{name}_dram"] = a
        aps[name] = nc.dram_tensor(f"in_{name}_dram", a.shape, _mybir.dt.from_np(a.dtype), kind="ExternalInput").ap()
    aps["out"] = nc.dram_tensor("out_0_dram", inputs["x"].shape, _mybir.dt.from_np(_np.dtype("float32")),
                                kind="ExternalOutput").ap()
    gnn_stack_kernel(nc, aps["x"], aps["adj"], aps)
    r = _run(nc, [arrays], core_ids=[0])
    return r.results[0]["out_0_dram"]
```

```python
from contextlib import ExitStack

import numpy as np

import concourse.bass as bass
from concourse import mybir

F32 = mybir.dt.float32
F32R = mybir.dt.float32r
ALU = mybir.AluOpType
ACT = mybir.ActivationFunctionType
AX_X = mybir.AxisListType.X


def gnn_stack_kernel(nc, x, adj, w):
    GRAPHS, N, D = x.shape
    PAIRS = GRAPHS // 2
    C = D // 128
    HEADS = 8
    HD = D // HEADS
    R = 128 // HD
    EPS = 1e-5
    ALPHA = 0.2
    QSCALE = float(HD) ** -0.5
    out = w["out"]
    assert N == 128 and C == 2 and HD == 32 and GRAPHS % 2 == 0

    with ExitStack() as ctx:
        def sb(name, shape, dt=F32):
            return ctx.enter_context(nc.sbuf_tensor(name, shape, dt))

        def sem(name):
            return ctx.enter_context(nc.semaphore(name))

        bank = [ctx.enter_context(nc.psum_tensor(f"bank{i}", [128, 512], F32)) for i in range(8)]

        xs = sb("xs", [128, GRAPHS, D])
        ident = sb("ident", [128, 128])
        ones = sb("ones", [128, 128])
        adj_sb = sb("adj_sb", [128, N])
        m_qk = [sb(f"m_qk{k}", [128, C, D], F32R) for k in range(2)]
        wv0T = [sb(f"wv0T{k}", [128, C, D], F32R) for k in range(2)]
        w1 = sb("w1", [128, C, D + 1])
        wa2 = sb("wa2", [128, C, N])
        beta = sb("beta", [128, 1])
        nadjT = sb("nadjT", [128, N])
        w2 = [sb(f"w2_{k}", [128, C, D], F32R) for k in range(2)]
        rows = sb("rows", [128, 3, D])
        mbias = sb("mbias", [128, N])
        wq3 = [sb(f"wq3_{k}", [128, C, D], F32R) for k in range(2)]
        wk3 = [sb(f"wk3_{k}", [128, C, D], F32R) for k in range(2)]
        wv3 = [sb(f"wv3_{k}", [128, C, D], F32R) for k in range(2)]
        wo3 = [sb(f"wo3_{k}", [128, C, D], F32R) for k in range(2)]
        bq = sb("bq", [128, C])
        bk = sb("bk", [128, C])
        mhalf = sb("mhalf", [128, 2])
        stats = sb("stats", [128, 2, 2, 6])
        mv = sb("mv", [128, 2, 2, 2])
        vare = sb("vare", [128, 2, 2])
        nmean = sb("nmean", [128, 2, 2])
        rstd = sb("rstd", [128, 2, 2])
        shift = sb("shift", [128, 2, 2])
        xn = sb("xn", [128, 2, D])
        xn2 = sb("xn2", [128, 2, D])
        hT = sb("hT", [128, C, 2, N])
        hTs = [sb(f"hTs{k}", [128, C, 2, N], F32R) for k in range(2)]
        yTs = [[sb(f"yTs{b}{k}", [128, C, 2, N], F32R) for k in range(2)] for b in range(2)]
        tT = sb("tT", [128, C, 2, N])
        val = sb("val", [128, 2, D + 1])
        val1 = sb("val1", [128, 2, D + 1])
        relm = sb("relm", [128, 2, N])
        relsq = sb("relsq", [128, 2, N])
        norm2 = sb("norm2", [128, 2])
        rnorm = sb("rnorm", [128, 2])
        wide = [sb(f"wide{g}", [128, HEADS, N]) for g in range(2)]
        prob = [sb(f"prob{g}", [128, HEADS, N]) for g in range(2)]
        probT = sb("probT", [128, HEADS, N])
        qT = sb("qT", [128, C, 2, N])
        kT = sb("kT", [128, C, 2, N])
        small = sb("small", [128, 64])
        oTs = [sb(f"oTs{k}", [128, 2, C, N], F32R) for k in range(2)]
        adj_pair = adj_sb[:, :].unsqueeze(1).to_broadcast([128, 2, N])
        mbias_pair = mbias[:, :].unsqueeze(1).to_broadcast([128, 2, N])

        def x_of(p, g):
            return xs[:, bass.ds(2 * p + g, 1), :].rearrange("p a d -> p (a d)")

        def x_pair(p):
            return xs[:, bass.ds(2 * p, 2), :]

        def since(n):
            return max(n, 0) if isinstance(n, int) else n

        def moments(dve, p, dve_step, b=0):
            for g in range(2):
                ins = nc.vector.bn_stats(stats[:, b, g, :], x_of(p, g))
            ins.then_inc(dve_step, 1)

        def mean_variance(dve, p, dve_step, b=0):
            dve.wait_ge(dve_step, 1)
            dve.wait_ge(dve_step, 2 * p + 1)
            for g in range(2):
                ins = nc.vector.bn_aggr(mv[:, b, g, :], stats[:, b, g, :])
            ins.then_inc(dve_step, 1)

        def root_argument(dve, p, dve_step, stats_ready, b=0):
            dve.wait_ge(dve_step, 2 * p + 2)
            nc.vector.tensor_scalar(nmean[:, b, :], mv[:, b, :, 0], -1.0, None, ALU.mult)
            nc.vector.tensor_scalar(vare[:, b, :], mv[:, b, :, 1], EPS, None, ALU.add).then_inc(stats_ready, 1)

        def layer_norm_stats(dve, p, dve_step, stats_ready, b=0):
            moments(dve, p, dve_step, b)
            mean_variance(dve, p, dve_step, b)
            root_argument(dve, p, dve_step, stats_ready, b)

        def inverse_root(pool, p, stats_ready, rstd_ready, b=0):
            pool.wait_ge(stats_ready, p + 1)
            nc.gpsimd.tensor_tensor(rstd[:, b, :], vare[:, b, :], mhalf[:, :], ALU.pow).then_inc(rstd_ready, 1)

        def root_and_shift(pool, p, stats_ready, rstd_ready, shift_ready, b=0):
            inverse_root(pool, p, stats_ready, rstd_ready, b)
            pool.wait_ge(rstd_ready, p + 1)
            nc.gpsimd.tensor_tensor(shift[:, b, :], nmean[:, b, :], rstd[:, b, :], ALU.mult).then_inc(shift_ready, 1)

        wld = sem("c_weights_loaded")
        c_id0, c_id1, c_ident, c_ones = sem("c_id0"), sem("c_id1"), sem("c_ident"), sem("c_ones")
        c_high = sem("c_high")
        c_root, c_mhalf = sem("c_root"), sem("c_mhalf")
        c_pe, c_dve, c_step = sem("c_pe"), sem("c_dve"), sem("c_step")
        with ExitStack() as cctx:
            wq0 = cctx.enter_context(nc.sbuf_tensor("wq0", [128, C, D], F32))
            wk0 = cctx.enter_context(nc.sbuf_tensor("wk0", [128, C, D], F32))
            wv0 = cctx.enter_context(nc.sbuf_tensor("wv0", [128, C, D], F32))
            w1T = cctx.enter_context(nc.sbuf_tensor("w1T", [128, C, D], F32))
            a12 = cctx.enter_context(nc.sbuf_tensor("a12", [128, 2, C], F32))
            row1 = cctx.enter_context(nc.sbuf_tensor("row1", [1, 3 * D + 2], F32))
            deg = cctx.enter_context(nc.sbuf_tensor("deg", [128, 6], F32))
            adjn = cctx.enter_context(nc.sbuf_tensor("adjn", [128, N], F32))
            raw = [cctx.enter_context(nc.sbuf_tensor(f"raw{k}", [128, C, D], F32)) for k in range(5)]

            with nc.Block() as block:
                @block.sync
                def _(sp):
                    w1_cols = w1[:, :, 0:D]
                    for dst, src in ((wq0, w["L0_gnn_Wq"]), (wk0, w["L0_gnn_Wk"]), (wv0, w["L0_gnn_Wv"]),
                                     (w1_cols, w["L1_gnn_W"]), (raw[0], w["L2_gnn_weight"]),
                                     (raw[1], w["L3_gnn_Wq"]), (raw[2], w["L3_gnn_Wk"]), (raw[3], w["L3_gnn_Wv"]),
                                     (raw[4], w["L3_gnn_Wo"])):
                        sp.dma_start(dst if dst is w1_cols else dst[:, :, :], src.rearrange("(c p) n -> p c n", p=128)).then_inc(wld, 16)
                    sp.dma_start(adj_sb[:, :], adj).then_inc(wld, 16)
                    with nc.allow_non_contiguous_dma("columns of small vectors"):
                        sp.dma_start(a12[:, :, :].rearrange("p k c -> p (k c)"), w["L1_gnn_a"].rearrange("(k p) o -> p (k o)", p=128)).then_inc(wld, 16)
                        sp.dma_start(bq[:, :], w["L3_gnn_bq"].rearrange("(c p) -> p c", p=128)).then_inc(wld, 16)
                        sp.dma_start(bk[:, :], w["L3_gnn_bk"].rearrange("(c p) -> p c", p=128)).then_inc(wld, 16)
                    for k, name in enumerate(("L2_gnn_bias", "L3_gnn_bv", "L3_gnn_bo")):
                        sp.dma_start(row1[0:1, k * D:(k + 1) * D], w[name].rearrange("(o n) -> o n", o=1)).then_inc(wld, 16)
                    sp.dma_start(row1[0:1, 3 * D:3 * D + 1], w["L1_gnn_beta"].rearrange("(o n) -> o n", o=1)).then_inc(wld, 16)

                LOADED = 16 * 17
                splits = [(m_qk, bank[0][:, :].rearrange("p (c n) -> p c n", c=C)),
                          (wv0T, bank[3][:, :].rearrange("p (c n) -> p c n", c=C))]
                splits += [(parts, raw[k][:, :, :]) for k, parts in enumerate((w2, wq3, wk3, wv3, wo3))]

                @block.gpsimd
                def _(pool):
                    nc.gpsimd.memset(ones[:, :], 1.0).then_inc(c_ones, 1)
                    nc.gpsimd.memset(mhalf[:, :], -0.5).then_inc(c_mhalf, 1)
                    nc.gpsimd.memset(ident[:, :], 0.0).then_inc(c_id0, 1)
                    pool.wait_ge(c_id0, 1)
                    nc.gpsimd.affine_select(out=ident[:, :], in_=ident[:, :], compare_op=ALU.not_equal, fill=1.0,
                                            base=0, pattern=[[-1, 128]], channel_multiplier=1).then_inc(c_ident, 1)
                    pool.wait_ge(c_mhalf, 1)
                    pool.wait_ge(c_step, 2)
                    nc.gpsimd.tensor_tensor(deg[:, 4:5], deg[:, 2:3], mhalf[:, 0:1], ALU.pow).then_inc(c_root, 1)

                @block.tensor
                def _(pe):
                    pe.wait_ge(wld, LOADED)
                    pe.wait_ge(c_ones, 1)
                    for d in range(C):
                        for e in range(C):
                            ins = nc.tensor.matmul(bank[0][:, d * D:(d + 1) * D], wq0[:, e, d * 128:(d + 1) * 128],
                                                   wk0[:, e, :], start=(e == 0), stop=(e == C - 1))
                    ins.then_inc(c_pe, 1)
                    for k in range(3):
                        ins = nc.tensor.matmul(bank[1 + k // 2][:, (k % 2) * D:(k % 2 + 1) * D], ones[0:1, :],
                                               row1[0:1, k * D:(k + 1) * D], start=True, stop=True)
                    ins = nc.tensor.matmul(bank[2][:, D:D + 1], ones[0:1, :], row1[0:1, 3 * D:3 * D + 1],
                                           start=True, stop=True)
                    ins.then_inc(c_pe, 1)
                    pe.wait_ge(c_ident, 1)
                    for k, src in enumerate((wv0, w1)):
                        for c in range(C):
                            for e in range(C):
                                ins = nc.tensor.transpose(bank[3 + k][:, c * D + e * 128:c * D + (e + 1) * 128],
                                                          src[:, e, c * 128:(c + 1) * 128], ident[:, :])
                    ins.then_inc(c_pe, 1)
                    pe.wait_ge(c_dve, 1)
                    for c in range(C):
                        for f in range(C):
                            ins = nc.tensor.matmul(bank[5][:, 2 * c:2 * c + 2], w1T[:, f, c * 128:(c + 1) * 128],
                                                   a12[:, :, f], start=(f == 0), stop=(f == C - 1))
                    ins.then_inc(c_pe, 1)
                    pe.wait_ge(c_dve, 2)
                    nc.tensor.transpose(bank[6][:, 0:N], adjn[:, :], ident[:, :]).then_inc(c_pe, 1)

                @block.vector
                def _(dve):
                    dve.wait_ge(wld, LOADED)
                    dve.wait_ge(c_ones, 1)
                    dve.wait_ge(c_pe, 3)
                    nc.vector.tensor_copy(w1T[:, :, :], bank[4][:, :].rearrange("p (c n) -> p c n", c=C)).then_inc(c_dve, 1)
                    nc.vector.tensor_copy(rows[:, 0:2, :], bank[1][:, :].rearrange("p (c n) -> p c n", c=2))
                    nc.vector.tensor_copy(rows[:, 2, :], bank[2][:, 0:D])
                    nc.vector.tensor_copy(beta[:, :], bank[2][:, D:D + 1])
                    nc.vector.tensor_scalar(mbias[:, :], adj_sb[:, :], -1.0, 1e9, ALU.add, ALU.mult)
                    nc.vector.tensor_scalar(bq[:, :], bq[:, :], QSCALE, None, ALU.mult)
                    nc.vector.tensor_reduce(deg[:, 0:1], adj_sb[:, :], AX_X, ALU.add).then_inc(c_step, 1)
                    dve.wait_ge(c_step, 1)
                    nc.vector.tensor_scalar(deg[:, 1:2], deg[:, 0:1], 0.0, None, ALU.is_gt)
                    nc.vector.tensor_scalar(deg[:, 2:3], deg[:, 0:1], float(np.finfo(np.float32).tiny), None,
                                            ALU.max).then_inc(c_step, 1)
                    dve.wait_ge(c_root, 1)
                    nc.vector.tensor_tensor(deg[:, 3:4], deg[:, 1:2], deg[:, 4:5], ALU.mult).then_inc(c_step, 1)
                    dve.wait_ge(c_step, 3)
                    nc.vector.tensor_scalar(adjn[:, :], adj_sb[:, :], deg[:, 3:4], None, ALU.mult).then_inc(c_dve, 1)
                    dve.wait_ge(c_pe, 5)
                    nc.vector.tensor_copy(w1[:, :, D:D + 1], bank[5][:, 0:2 * C:2].unsqueeze(2))
                    for c in range(C):
                        nc.vector.tensor_scalar(wa2[:, c, :], ones[:, :], bank[5][:, 2 * c + 1:2 * c + 2], None, ALU.mult)
                    nc.vector.tensor_scalar(nadjT[:, :], bank[6][:, 0:N], deg[:, 3:4], None, ALU.mult).then_inc(c_dve, 1)
                    for k, (parts, src) in enumerate(splits):
                        dve.wait_ge(c_high, k + 1)
                        nc.vector.tensor_tensor(parts[1][:, :, :], src, parts[0][:, :, :].bitcast(F32), ALU.subtract)
                    dve.wait_ge(c_dve, 3)

                @block.scalar
                def _(act):
                    act.wait_ge(wld, LOADED)
                    act.wait_ge(c_pe, 3)
                    for parts, src in splits:
                        nc.scalar.copy(parts[0][:, :, :], src).then_inc(c_high, 1)


        def transposes(pe_ps):
            for c in range(C):
                for g in range(2):
                    ins = nc.tensor.transpose(pe_ps[:, c * 2 * N + g * N:c * 2 * N + (g + 1) * N],
                                              xn[:, g, c * 128:(c + 1) * 128], ident[:, :])
            return ins

        def node_product(ps_g, weight, g):
            for c in range(C):
                ins = nc.tensor.matmul(ps_g, hT[:, c, g, :], weight[:, c, :], start=(c == 0), stop=(c == C - 1))
            return ins

        PARTS = ((0, 0), (0, 1), (1, 0))

        def split_product(ps, lhsT, rhs):
            terms = [(a, b, c) for c in range(C) for a, b in PARTS]
            for n, (a, b, c) in enumerate(terms):
                ins = nc.tensor.matmul(ps, lhsT(a, c), rhs(b, c), start=(n == 0), stop=(n == len(terms) - 1))
            return ins

        def node_split_product(ps_g, weight, g):
            return split_product(ps_g, lambda k, c: hTs[k][:, c, g, :], lambda k, c: weight[k][:, c, :])

        def feature_product(ps, weight):
            for m in range(C):
                ins = split_product(ps[:, m * 2 * N:(m + 1) * 2 * N],
                                    lambda k, c: weight[k][:, c, m * 128:(m + 1) * 128],
                                    lambda k, c: hTs[k][:, c, :, :].rearrange("p g n -> p (g n)"))
            return ins

        hT_high = hTs[0][:, :, :, :].rearrange("p c g n -> p (c g n)")
        hT_low = hTs[1][:, :, :, :].rearrange("p c g n -> p (c g n)")
        hT_flat = hT[:, :, :, :].rearrange("p c g n -> p (c g n)")

        x_loaded = sem("l0_x_loaded")
        xn_ready, tr_done, hT_ready = sem("l0_xn_ready"), sem("l0_tr_done"), sem("l0_hT_ready")
        t_done, tT_ready, v_done, v_ready = sem("l0_t_done"), sem("l0_tT_ready"), sem("l0_v_done"), sem("l0_v_ready")
        rel_done, relm_ready, relsq_ready = sem("l0_rel_done"), sem("l0_relm_ready"), sem("l0_relsq_ready")
        n2_ready, rn_ready = sem("l0_norm2_ready"), sem("l0_rnorm_ready")
        high_ready, low_ready = sem("l0_high_ready"), sem("l0_low_ready")
        stats_ready, rstd_ready = sem("l0_stats_ready"), sem("l0_rstd_ready")
        out_done, x_done, dstep = sem("l0_out_done"), sem("l0_x_done"), sem("l0_dve_step")
        HT, TT, VV, RR, NO, OO = bank[0:6]

        with nc.Block() as block:
            @block.sync
            def _(sp):
                sp.dma_start(xs[:, 0:2, :], x[0:2, :, :].rearrange("g n d -> n g d")).then_inc(x_loaded, 16)
                with sp.Fori(1, PAIRS) as p:
                    sp.wait_ge(x_loaded, 16 * p)
                    sp.dma_start(x_pair(p), x[bass.ds(2 * p, 2), :, :].rearrange("g n d -> n g d")).then_inc(x_loaded, 16)

            @block.tensor
            def _(pe):
                def turn(p):
                    pe.wait_ge(xn_ready, p + 1)
                    pe.wait_ge(hT_ready, since(p))
                    transposes(HT).then_inc(tr_done, 1)

                def t_product(p):
                    pe.wait_ge(low_ready, p + 1)
                    feature_product(TT, m_qk).then_inc(t_done, 1)

                def values(p):
                    pe.wait_ge(v_ready, since(p))
                    for g in range(2):
                        ins = node_split_product(VV[:, g * D:(g + 1) * D], wv0T, g)
                    ins.then_inc(v_done, 1)

                def relation(p):
                    pe.wait_ge(tT_ready, p + 1)
                    pe.wait_ge(hT_ready, p + 1)
                    pe.wait_ge(relm_ready, since(p))
                    for g in range(2):
                        for c in range(C):
                            ins = nc.tensor.matmul(RR[:, g * N:(g + 1) * N], hT[:, c, g, :], tT[:, c, g, :],
                                                   start=(c == 0), stop=(c == C - 1))
                    ins.then_inc(rel_done, 1)

                def outputs(p):
                    pe.wait_ge(relsq_ready, p + 1)
                    pe.wait_ge(x_done, since(p))
                    for g in range(2):
                        nc.tensor.matmul(NO[:, g:g + 1], relsq[:, g, :], ones[:, 0:1], start=True, stop=True)
                    pe.wait_ge(v_ready, p + 1)
                    for g in range(2):
                        ins = nc.tensor.matmul(OO[:, g * D:(g + 1) * D], relm[:, g, :], val[:, g, 0:D], start=True, stop=True)
                    ins.then_inc(out_done, 1)

                turn(0)
                t_product(0)
                turn(1)
                values(0)
                relation(0)

                def step(p):
                    t_product(p)
                    turn(p + 1)
                    values(p)
                    relation(p)
                    outputs(p - 1)

                step(1)
                with pe.Fori(2, PAIRS - 1) as p:
                    step(p)
                t_product(PAIRS - 1)
                values(PAIRS - 1)
                relation(PAIRS - 1)
                outputs(PAIRS - 2)
                outputs(PAIRS - 1)

            @block.scalar
            def _(act):
                def relu_high(p):
                    act.wait_ge(tr_done, p + 1)
                    act.wait_ge(v_done, since(p))
                    nc.scalar.activation(hT_high, HT[:, :], ACT.Relu).then_inc(high_ready, 1)

                def relu_T(p):
                    act.wait_ge(low_ready, p + 1)
                    act.wait_ge(rel_done, since(p))
                    nc.scalar.activation(hT_flat, HT[:, :], ACT.Relu).then_inc(hT_ready, 1)

                def copy_t(p):
                    act.wait_ge(t_done, p + 1)
                    nc.scalar.copy(tT[:, :, :, :].rearrange("p c g n -> p (c g n)"), TT[:, :]).then_inc(tT_ready, 1)

                def copy_v(p):
                    act.wait_ge(v_done, p + 1)
                    act.wait_ge(out_done, since(p))
                    nc.scalar.copy(val[:, :, 0:D], VV[:, :].rearrange("p (g n) -> p g n", g=2)).then_inc(v_ready, 1)

                relu_high(0)
                relu_T(0)
                copy_t(0)
                relu_high(1)
                copy_v(0)
                relu_T(1)
                with act.Fori(1, PAIRS - 1) as p:
                    copy_t(p)
                    relu_high(p + 1)
                    relu_T(p + 1)
                    copy_v(p)
                copy_t(PAIRS - 1)
                copy_v(PAIRS - 1)

            @block.gpsimd
            def _(pool):
                def squares(p):
                    pool.wait_ge(relm_ready, p + 1)
                    nc.gpsimd.tensor_tensor(relsq[:, :, :], relm[:, :, :], relm[:, :, :], ALU.mult).then_inc(relsq_ready, 1)

                def inverse_norm(p):
                    pool.wait_ge(n2_ready, p + 1)
                    nc.gpsimd.tensor_tensor(rnorm[:, :], norm2[:, :], mhalf[:, :], ALU.pow).then_inc(rn_ready, 1)

                for p in range(3):
                    inverse_root(pool, p, stats_ready, rstd_ready)
                inverse_root(pool, 3, stats_ready, rstd_ready)
                squares(0)
                with pool.Fori(1, PAIRS - 3) as p:
                    squares(p)
                    inverse_norm(p - 1)
                    inverse_root(pool, p + 3, stats_ready, rstd_ready)
                for p in range(PAIRS - 3, PAIRS):
                    squares(p)
                    inverse_norm(p - 1)
                inverse_norm(PAIRS - 1)

            @block.vector
            def _(dve):
                def statistics(p):
                    dve.wait_ge(x_loaded, 16 * p + 16)
                    layer_norm_stats(dve, p, dstep, stats_ready)

                def normalise(p):
                    dve.wait_ge(rstd_ready, p + 1)
                    dve.wait_ge(tr_done, since(p))
                    for g in range(2):
                        ins = nc.vector.tensor_scalar(xn[:, g, :], x_of(p, g), mv[:, 0, g, 0:1], rstd[:, 0, g:g + 1],
                                                      ALU.subtract, ALU.mult)
                    ins.then_inc(xn_ready, 1)

                def low_part(p):
                    dve.wait_ge(high_ready, p + 1)
                    nc.vector.scalar_tensor_tensor(hT_low, HT[:, :], 0.0, hT_high.bitcast(F32), ALU.max,
                                                   ALU.subtract).then_inc(low_ready, 1)

                def mask(p):
                    dve.wait_ge(rel_done, p + 1)
                    dve.wait_ge(out_done, since(p))
                    nc.vector.tensor_tensor(relm[:, :, :], RR[:, 0:2 * N].rearrange("p (g n) -> p g n", g=2),
                                            adj_pair, ALU.mult).then_inc(relm_ready, 1)

                def copy_norm2(p):
                    dve.wait_ge(out_done, p + 1)
                    nc.vector.tensor_copy(norm2[:, :], NO[:, 0:2]).then_inc(n2_ready, 1)

                def update(p):
                    dve.wait_ge(rn_ready, p + 1)
                    for g in range(2):
                        ins = nc.vector.scalar_tensor_tensor(x_of(p, g), OO[:, g * D:(g + 1) * D], rnorm[:, g:g + 1],
                                                             x_of(p, g), ALU.mult, ALU.add)
                    ins.then_inc(x_done, 1)

                for p in range(2):
                    statistics(p)
                    normalise(p)
                    low_part(p)
                statistics(2)
                normalise(2)
                statistics(3)
                mask(0)

                with dve.Fori(1, PAIRS - 3) as p:
                    low_part(p + 1)
                    mask(p)
                    normalise(p + 2)
                    copy_norm2(p - 1)
                    statistics(p + 3)
                    update(p - 1)
                for p in range(PAIRS - 3, PAIRS):
                    if p + 1 < PAIRS:
                        low_part(p + 1)
                    mask(p)
                    if p + 2 < PAIRS:
                        normalise(p + 2)
                    copy_norm2(p - 1)
                    update(p - 1)
                copy_norm2(PAIRS - 1)
                update(PAIRS - 1)
                dve.wait_ge(x_done, PAIRS)

        xn_ready, tr_done, hT_ready = sem("l1_xn_ready"), sem("l1_tr_done"), sem("l1_hT_ready")
        h_done, val_ready, e_done = sem("l1_h_done"), sem("l1_val_ready"), sem("l1_e_done")
        e_ready, em_ready, nmax_ready = sem("l1_e_ready"), sem("l1_em_ready"), sem("l1_nmax_ready")
        prob_ready, pt_done, pt_ready, att_done = sem("l1_prob_ready"), sem("l1_pt_done"), sem("l1_pt_ready"), sem("l1_att_done")
        rinv_ready, bh_ready, u_ready, umin_ready = sem("l1_rinv_ready"), sem("l1_bh_ready"), sem("l1_u_ready"), sem("l1_umin_ready")
        eu_ready, elu_ready, x_done, dstep = sem("l1_eu_ready"), sem("l1_elu_ready"), sem("l1_x_done"), sem("l1_dve_step")
        leaky_ready = sem("l1_leaky_ready")
        stats_ready, rstd_ready, shift_ready = sem("l1_stats_ready"), sem("l1_rstd_ready"), sem("l1_shift_ready")
        HT, HG, PT, EE, UU = bank[0], (bank[1], bank[2]), bank[3], bank[4], bank[5]
        valb = [val, val1]
        bh = [wide[b][:, 0:4, :].rearrange("p a n -> p (a n)").rearrange("p (g d) -> p g d", g=2) for b in range(2)]
        u_sb = wide[0][:, 4:8, :].rearrange("p a n -> p (a n)")
        umin = wide[1][:, 4:8, :].rearrange("p a n -> p (a n)")
        eu = prob[0][:, 0:4, :].rearrange("p a n -> p (a n)")
        elu = prob[0][:, 4:8, :].rearrange("p a n -> p (a n)")
        e_sb, em, p1, p1T = (prob[1][:, 2 * k:2 * k + 2, :] for k in range(4))
        el = tT[:, 1, :, :]
        nmax, rsum, rinv = small[:, 0:2], small[:, 2:4], small[:, 4:6]

        with nc.Block() as block:
            @block.tensor
            def _(pe):
                def turn(p):
                    pe.wait_ge(xn_ready, p + 1)
                    transposes(HT).then_inc(tr_done, 1)

                def product(p):
                    pe.wait_ge(hT_ready, p + 1)
                    pe.wait_ge(val_ready, since(p))
                    for g in range(2):
                        ins = node_product(HG[g][:, 0:D + 1], w1, g)
                    ins.then_inc(h_done, 1)

                def turn_prob(p):
                    pe.wait_ge(prob_ready, p + 1)
                    pe.wait_ge(pt_ready, since(p))
                    for g in range(2):
                        ins = nc.tensor.transpose(PT[:, g * N:(g + 1) * N], p1[:, g, :], ident[:, :])
                    ins.then_inc(pt_done, 1)

                def spread(p):
                    pe.wait_ge(e_ready, since(p))
                    for c in range(C):
                        ins = nc.tensor.matmul(EE[:, 0:2 * N], wa2[:, c, :], hT[:, c, :, :].rearrange("p g n -> p (g n)"),
                                               start=(c == 0), stop=(c == C - 1))
                    ins.then_inc(e_done, 1)

                def attend(p, b):
                    pe.wait_ge(pt_ready, p + 1)
                    pe.wait_ge(u_ready, since(p))
                    for g in range(2):
                        ins = nc.tensor.matmul(UU[:, g * D:(g + 1) * D], p1T[:, g, :], valb[b][:, g, 0:D], start=True, stop=True)
                    ins.then_inc(att_done, 1)

                def step(p, b, first=False, last=False):
                    product(p)
                    if not first:
                        turn_prob(p - 1)
                    spread(p)
                    if not last:
                        turn(p + 1)
                    if not first:
                        attend(p - 1, 1 - b)

                turn(0)
                step(0, 0, first=True)
                step(1, 1)
                with pe.Fori(1, PAIRS // 2 - 1) as j:
                    for b in range(2):
                        step(2 * j + b, b)
                step(PAIRS - 2, 0)
                step(PAIRS - 1, 1, last=True)
                turn_prob(PAIRS - 1)
                attend(PAIRS - 1, 1)

            @block.scalar
            def _(act):
                def normalise(p, b):
                    act.wait_ge(shift_ready, p + 1)
                    act.wait_ge(tr_done, since(p))
                    for g in range(2):
                        ins = nc.scalar.activation(xn[:, g, :], x_of(p, g), ACT.Relu, bias=shift[:, b, g:g + 1],
                                                   scale=rstd[:, b, g:g + 1])
                    ins.then_inc(xn_ready, 1)

                def copy_hT(p):
                    act.wait_ge(tr_done, p + 1)
                    act.wait_ge(e_done, since(p))
                    nc.scalar.copy(hT_flat, HT[:, :]).then_inc(hT_ready, 1)

                def copy_h(p, b):
                    act.wait_ge(h_done, p + 1)
                    act.wait_ge(att_done, since(p - 1))
                    act.wait_ge(bh_ready, since(p - 1))
                    for g in range(2):
                        ins = nc.scalar.copy(valb[b][:, g, :], HG[g][:, 0:D + 1])
                    ins.then_inc(val_ready, 1)

                def add_s1(p, b):
                    act.wait_ge(e_done, p + 1)
                    act.wait_ge(leaky_ready, since(p))
                    act.wait_ge(val_ready, p + 1)
                    for g in range(2):
                        ins = nc.scalar.activation(e_sb[:, g, :], EE[:, g * N:(g + 1) * N], ACT.Identity,
                                                   bias=valb[b][:, g, D:D + 1])
                    ins.then_inc(e_ready, 1)

                def softmax_exp(p):
                    act.wait_ge(nmax_ready, p + 1)
                    act.wait_ge(pt_done, since(p))
                    act.wait_ge(rinv_ready, since(p))
                    for g in range(2):
                        ins = nc.scalar.activation(p1[:, g, :], em[:, g, :], ACT.Exp, bias=nmax[:, g:g + 1],
                                                   accum_out=rsum[:, g:g + 1])
                    ins.then_inc(prob_ready, 1)

                def elu_exp(p):
                    act.wait_ge(umin_ready, p + 1)
                    act.wait_ge(elu_ready, since(p))
                    nc.scalar.activation(eu, umin, ACT.Exp).then_inc(eu_ready, 1)

                def step(p, b, lag=2, last=False, norms=True):
                    copy_h(p, b)
                    if lag >= 2:
                        elu_exp(p - 2)
                    add_s1(p, b)
                    if not last:
                        copy_hT(p + 1)
                    if norms:
                        normalise(p + 2, b)
                    softmax_exp(p)

                normalise(0, 0)
                copy_hT(0)
                normalise(1, 1)
                step(0, 0, lag=0)
                step(1, 1, lag=1)
                step(2, 0)
                step(3, 1)
                with act.Fori(2, PAIRS // 2 - 1) as j:
                    for b in range(2):
                        step(2 * j + b, b)
                step(PAIRS - 2, 0, norms=False)
                step(PAIRS - 1, 1, last=True, norms=False)
                elu_exp(PAIRS - 2)
                elu_exp(PAIRS - 1)

            @block.gpsimd
            def _(pool):
                def beta_h(p, b):
                    pool.wait_ge(val_ready, p + 1)
                    pool.wait_ge(u_ready, since(p - 1))
                    nc.gpsimd.tensor_tensor(bh[b], valb[b][:, :, 0:D], beta[:, :].unsqueeze(2).to_broadcast([128, 2, D]), ALU.mult).then_inc(bh_ready, 1)

                def add(p):
                    pool.wait_ge(elu_ready, p + 1)
                    nc.gpsimd.tensor_tensor(x_pair(p), x_pair(p), elu.rearrange("p (g d) -> p g d", g=2),
                                            ALU.add).then_inc(x_done, 1)

                def step(p, b, lag=2, norms=True):
                    beta_h(p, b)
                    if norms:
                        root_and_shift(pool, p + 3, stats_ready, rstd_ready, shift_ready, 1 - b)
                    if lag >= 2:
                        add(p - 2)

                for p in range(3):
                    root_and_shift(pool, p, stats_ready, rstd_ready, shift_ready, p % 2)
                step(0, 0, lag=0)
                step(1, 1, lag=1)
                with pool.Fori(1, PAIRS // 2 - 2) as j:
                    for b in range(2):
                        step(2 * j + b, b)
                for p in range(PAIRS - 4, PAIRS):
                    step(p, p % 2, norms=p + 3 < PAIRS)
                add(PAIRS - 2)
                add(PAIRS - 1)

            @block.vector
            def _(dve):
                def norm(p, b):
                    dve.wait_ge(xn_ready, since(p - 1))
                    layer_norm_stats(dve, p, dstep, stats_ready, b)

                def copy_pT(p):
                    dve.wait_ge(pt_done, p + 1)
                    dve.wait_ge(att_done, since(p))
                    nc.vector.tensor_copy(p1T, PT[:, 0:2 * N].rearrange("p (g n) -> p g n", g=2)).then_inc(pt_ready, 1)
                    nc.vector.reciprocal(rinv, rsum).then_inc(rinv_ready, 1)

                def elu_max(p):
                    dve.wait_ge(eu_ready, p + 1)
                    dve.wait_ge(x_done, since(p))
                    nc.vector.scalar_tensor_tensor(elu, eu, -1.0, u_sb, ALU.add, ALU.max).then_inc(elu_ready, 1)

                def mask_max(p):
                    dve.wait_ge(e_ready, p + 1)
                    nc.vector.scalar_tensor_tensor(el, e_sb, ALPHA, e_sb, ALU.mult, ALU.max).then_inc(leaky_ready, 1)
                    dve.wait_ge(leaky_ready, p + 1)
                    dve.wait_ge(prob_ready, since(p))
                    nc.vector.tensor_tensor(em, el, adj_pair, ALU.mult).then_inc(em_ready, 1)
                    dve.wait_ge(em_ready, p + 1)
                    nc.vector.tensor_reduce(nmax, em, AX_X, ALU.max, negate=True).then_inc(nmax_ready, 1)

                def gather(p, b):
                    dve.wait_ge(att_done, p + 1)
                    dve.wait_ge(bh_ready, p + 1)
                    dve.wait_ge(rinv_ready, p + 1)
                    dve.wait_ge(elu_ready, since(p))
                    for g in range(2):
                        ins = nc.vector.scalar_tensor_tensor(u_sb[:, g * D:(g + 1) * D], UU[:, g * D:(g + 1) * D],
                                                             rinv[:, g:g + 1], bh[b][:, g, :], ALU.mult, ALU.add)
                    ins.then_inc(u_ready, 1)
                    dve.wait_ge(u_ready, p + 1)
                    dve.wait_ge(eu_ready, since(p))
                    nc.vector.tensor_scalar(umin, u_sb, 0.0, None, ALU.min).then_inc(umin_ready, 1)

                def step(p, b, lag=2, norms=True):
                    if lag >= 2:
                        gather(p - 2, b)
                    if norms:
                        dve.wait_ge(xn_ready, p + 2)
                        moments(dve, p + 3, dstep, 1 - b)
                    if lag >= 1:
                        copy_pT(p - 1)
                    if norms:
                        mean_variance(dve, p + 3, dstep, 1 - b)
                        root_argument(dve, p + 3, dstep, stats_ready, 1 - b)
                    if lag >= 2:
                        elu_max(p - 2)
                    mask_max(p)

                norm(0, 0)
                norm(1, 1)
                norm(2, 0)
                step(0, 0, lag=0)
                step(1, 1, lag=1)
                step(2, 0)
                step(3, 1)
                with dve.Fori(2, PAIRS // 2 - 2) as j:
                    for b in range(2):
                        step(2 * j + b, b)
                for p in range(PAIRS - 4, PAIRS):
                    step(p, p % 2, norms=p + 3 < PAIRS)
                gather(PAIRS - 2, 0)
                copy_pT(PAIRS - 1)
                elu_max(PAIRS - 2)
                gather(PAIRS - 1, 1)
                elu_max(PAIRS - 1)

        xn_ready, yt_done, yt_ready, out_done = sem("l2_xn_ready"), sem("l2_yt_done"), sem("l2_yt_ready"), sem("l2_out_done")
        bias_done, x_done, dstep = sem("l2_bias_done"), sem("l2_x_done"), sem("l2_dve_step")
        stats_ready, rstd_ready, shift_ready = sem("l2_stats_ready"), sem("l2_rstd_ready"), sem("l2_shift_ready")
        high_ready = sem("l2_high_ready")
        YT, OO = bank[0:2], bank[2:4]
        xnb = [xn, xn2]
        yT_high = [yTs[b][0][:, :, :, :].rearrange("p c g n -> p (c g n)") for b in range(2)]
        yT_low = [yTs[b][1][:, :, :, :].rearrange("p c g n -> p (c g n)") for b in range(2)]

        with nc.Block() as block:
            @block.tensor
            def _(pe):
                def gather(p, b):
                    pe.wait_ge(xn_ready, p + 1)
                    pe.wait_ge(yt_ready, since(p - 1))
                    for c in range(C):
                        for g in range(2):
                            ins = nc.tensor.matmul(YT[b][:, (2 * c + g) * N:(2 * c + g + 1) * N],
                                                   xnb[b][:, g, c * 128:(c + 1) * 128], nadjT[:, :], start=True, stop=True)
                    ins.then_inc(yt_done, 1)

                def outputs(p, b):
                    pe.wait_ge(yt_ready, p + 1)
                    pe.wait_ge(x_done, since(p - 1))
                    for g in range(2):
                        ins = split_product(OO[b][:, g * D:(g + 1) * D], lambda k, c: yTs[b][k][:, c, g, :],
                                            lambda k, c: w2[k][:, c, :])
                    ins.then_inc(out_done, 1)

                gather(0, 0)
                for p in range(1, 4):
                    gather(p, p % 2)
                    outputs(p - 1, (p - 1) % 2)
                with pe.Fori(2, PAIRS // 2) as j:
                    for b in range(2):
                        gather(2 * j + b, b)
                        outputs(2 * j + b - 1, 1 - b)
                outputs(PAIRS - 1, 1)

            @block.scalar
            def _(act):
                def normalise(p, b):
                    act.wait_ge(shift_ready, p + 1)
                    act.wait_ge(yt_done, since(p - 1))
                    for g in range(2):
                        ins = nc.scalar.activation(xnb[b][:, g, :], x_of(p, g), ACT.Relu, bias=shift[:, b, g:g + 1],
                                                   scale=rstd[:, b, g:g + 1])
                    ins.then_inc(xn_ready, 1)

                def copy_high(p, b):
                    act.wait_ge(yt_done, p + 1)
                    act.wait_ge(out_done, since(p - 1))
                    nc.scalar.copy(yT_high[b], YT[b][:, :]).then_inc(high_ready, 1)

                normalise(0, 0)
                normalise(1, 1)
                for p in range(2):
                    copy_high(p, p)
                    normalise(p + 2, p)
                with act.Fori(1, PAIRS // 2 - 1) as j:
                    for b in range(2):
                        copy_high(2 * j + b, b)
                        normalise(2 * j + b + 2, b)
                copy_high(PAIRS - 2, 0)
                copy_high(PAIRS - 1, 1)

            @block.gpsimd
            def _(pool):
                def add_bias(p):
                    pool.wait_ge(xn_ready, p + 1)
                    nc.gpsimd.tensor_tensor(x_pair(p), x_pair(p), rows[:, 0:1, :].to_broadcast([128, 2, D]),
                                            ALU.add).then_inc(bias_done, 1)

                for p in range(3):
                    root_and_shift(pool, p, stats_ready, rstd_ready, shift_ready, p % 2)
                add_bias(0)
                root_and_shift(pool, 3, stats_ready, rstd_ready, shift_ready, 1)
                add_bias(1)
                with pool.Fori(2, PAIRS // 2) as j:
                    for b in range(2):
                        root_and_shift(pool, 2 * j + b, stats_ready, rstd_ready, shift_ready, b)
                        add_bias(2 * j + b - 2)
                add_bias(PAIRS - 2)
                add_bias(PAIRS - 1)

            @block.vector
            def _(dve):
                def norm(p, b):
                    dve.wait_ge(xn_ready, since(p - 1))
                    layer_norm_stats(dve, p, dstep, stats_ready, b)

                def low_part(p, b):
                    dve.wait_ge(high_ready, p + 1)
                    nc.vector.tensor_tensor(yT_low[b], YT[b][:, :], yT_high[b].bitcast(F32), ALU.subtract).then_inc(yt_ready, 1)

                def update(p, b):
                    dve.wait_ge(out_done, p + 1)
                    dve.wait_ge(bias_done, p + 1)
                    nc.vector.tensor_tensor(x_pair(p), OO[b][:, :].rearrange("p (g d) -> p g d", g=2), x_pair(p),
                                            ALU.add).then_inc(x_done, 1)

                def step(p, b, first=False, norms=True):
                    if norms:
                        dve.wait_ge(xn_ready, p + 2)
                        moments(dve, p + 3, dstep, 1 - b)
                    low_part(p, b)
                    if norms:
                        mean_variance(dve, p + 3, dstep, 1 - b)
                    if not first:
                        update(p - 2, b)
                    if norms:
                        root_argument(dve, p + 3, dstep, stats_ready, 1 - b)

                for p in range(3):
                    norm(p, p % 2)
                step(0, 0, first=True)
                step(1, 1, first=True)
                with dve.Fori(1, PAIRS // 2 - 2) as j:
                    for b in range(2):
                        step(2 * j + b, b)
                for p in range(PAIRS - 4, PAIRS):
                    step(p, p % 2, norms=p + 3 < PAIRS)
                update(PAIRS - 2, 0)
                update(PAIRS - 1, 1)

        xn_ready, tr_done = sem("l3_xn_ready"), sem("l3_tr_done")
        q_done, q_ready, k_done, k_ready = sem("l3_q_done"), sem("l3_q_ready"), sem("l3_k_done"), sem("l3_k_ready")
        v_done, v_ready, s_done, s_masked = sem("l3_v_done"), sem("l3_v_ready"), sem("l3_s_done"), sem("l3_s_masked")
        high_ready, low_ready, o_high_ready = sem("l3_high_ready"), sem("l3_low_ready"), sem("l3_o_high_ready")
        nmax_ready, exp_done, rinv_ready = sem("l3_nmax_ready"), sem("l3_exp_done"), sem("l3_rinv_ready")
        prob_ready, pt_done, pt_ready = sem("l3_prob_ready"), sem("l3_pt_done"), sem("l3_pt_ready")
        o_done, o_ready, y_done, x_done = sem("l3_o_done"), sem("l3_o_ready"), sem("l3_y_done"), sem("l3_x_done")
        stats_ready, rstd_ready = sem("l3_stats_ready"), sem("l3_rstd_ready")
        bias_done, dstep, stored = sem("l3_bias_done"), sem("l3_dve_step"), sem("l3_stored")
        SS, PT, OT, TQ = bank[0:4], bank[4:6], bank[6], bank[7]
        VV, KY = PT
        nmax = [small[:, 8 * g:8 * g + 8] for g in range(2)]
        rsum = [small[:, 24 + 8 * g:32 + 8 * g] for g in range(2)]
        rinv = [small[:, 40 + 8 * g:48 + 8 * g] for g in range(2)]

        with nc.Block() as block:
            @block.tensor
            def _(pe):
                def turn(p):
                    pe.wait_ge(xn_ready, p + 1)
                    pe.wait_ge(q_ready, since(p))
                    transposes(TQ).then_inc(tr_done, 1)

                def project_q(p):
                    pe.wait_ge(low_ready, p + 1)
                    feature_product(TQ, wq3).then_inc(q_done, 1)

                def project_k(p):
                    pe.wait_ge(pt_ready, since(4 * p - 2))
                    feature_product(KY, wk3).then_inc(k_done, 1)

                def project_v(t, g):
                    pe.wait_ge(pt_ready, since(2 * t - 3))
                    node_split_product(VV[:, 0:D], wv3, g).then_inc(v_done, 1)

                def scores(t, g):
                    for r in range(R):
                        pe.wait_ge(s_masked, since(R * t + r + 1 - R))
                        for c in range(C):
                            rows_r = slice(HD * r, HD * (r + 1))
                            ins = nc.tensor.matmul(SS[r][:, c * N:(c + 1) * N], qT[rows_r, c, g, :], kT[rows_r, c, g, :],
                                                   start=True, stop=True)
                        ins.then_inc(s_done, 1)

                def turn_prob(t, g, values, outputs):
                    for half in range(2):
                        pe.wait_ge(prob_ready, 2 * t + half + 1)
                        if half == 0:
                            pe.wait_ge(v_ready, values)
                        else:
                            pe.wait_ge(x_done, outputs)
                        for k in range(4):
                            ins = nc.tensor.transpose(PT[half][:, k * N:(k + 1) * N], prob[g][:, 4 * half + k, :], ident[:, :])
                        ins.then_inc(pt_done, 1)

                def attend(t, g):
                    pe.wait_ge(o_ready, since(t))
                    for half in range(2):
                        pe.wait_ge(pt_ready, 2 * t + half + 1)
                        for r in range(2 * half, 2 * half + 2):
                            for c in range(C):
                                h = c * R + r
                                ins = nc.tensor.matmul(OT[HD * r:HD * (r + 1), c * N:(c + 1) * N],
                                                       val[:, g, HD * h:HD * (h + 1)], probT[:, r * C + c, :], start=True, stop=True)
                    ins.then_inc(o_done, 1)

                def project_o(p):
                    pe.wait_ge(o_ready, 2 * p + 2)
                    for g in range(2):
                        ins = split_product(KY[:, g * D:(g + 1) * D], lambda k, c: oTs[k][:, g, c, :],
                                            lambda k, c: wo3[k][:, c, :])
                    ins.then_inc(y_done, 1)

                def pair(p, first=False, last=False):
                    pe.wait_ge(q_ready, p + 1)
                    pe.wait_ge(k_ready, p + 1)
                    scores(2 * p, 0)
                    if not first:
                        turn_prob(2 * p - 1, 1, 2 * p + 1, since(p - 1))
                    if not last:
                        turn(p + 1)
                    if not first:
                        attend(2 * p - 1, 1)
                    if first:
                        pe.wait_ge(v_ready, 1)
                    project_v(2 * p + 1, 1)
                    if not first:
                        project_o(p - 1)
                    scores(2 * p + 1, 1)
                    turn_prob(2 * p, 0, 2 * p + 2, since(p))
                    if not last:
                        project_q(p + 1)
                        project_k(p + 1)
                    attend(2 * p, 0)
                    if not last:
                        project_v(2 * p + 2, 0)

                turn(0)
                project_q(0)
                project_k(0)
                project_v(0, 0)
                pair(0, first=True)
                pair(1)
                with pe.Fori(2, PAIRS - 1) as p:
                    pair(p)
                pair(PAIRS - 1, last=True)
                turn_prob(2 * PAIRS - 1, 1, 2 * PAIRS, PAIRS - 1)
                attend(2 * PAIRS - 1, 1)
                project_o(PAIRS - 1)

            @block.scalar
            def _(act):
                def relu_high(p):
                    act.wait_ge(tr_done, p + 1)
                    act.wait_ge(v_done, since(2 * p))
                    nc.scalar.activation(hT_high, TQ[:, :], ACT.Relu).then_inc(high_ready, 1)

                def copy_q(p):
                    act.wait_ge(q_done, p + 1)
                    for c in range(C):
                        ins = nc.scalar.activation(qT[:, c, :, :].rearrange("p g n -> p (g n)"), TQ[:, c * 2 * N:(c + 1) * 2 * N],
                                                   ACT.Identity, bias=bq[:, c:c + 1], scale=QSCALE)
                    ins.then_inc(q_ready, 1)

                def exponentials(t, g, half, start=0, end=4):
                    act.wait_ge(nmax_ready, 2 * t + half + 1)
                    for k in range(4 * half + start, 4 * half + end):
                        ins = nc.scalar.activation(prob[g][:, k, :], wide[g][:, k, :], ACT.Exp, bias=nmax[g][:, k:k + 1],
                                                   accum_out=rsum[g][:, k:k + 1])
                    if end == 4:
                        ins.then_inc(exp_done, 1)

                def copy_pT(t):
                    for half in range(2):
                        act.wait_ge(pt_done, 2 * t + half + 1)
                        act.wait_ge(o_done, since(t))
                        nc.scalar.copy(probT[:, 4 * half:4 * half + 4, :].rearrange("p r n -> p (r n)"),
                                       PT[half][:, :]).then_inc(pt_ready, 1)

                def copy_o(t, g):
                    act.wait_ge(o_done, t + 1)
                    nc.scalar.copy(oTs[0][:, g, :, :].rearrange("p c n -> p (c n)"), OT[:, 0:D]).then_inc(o_high_ready, 1)

                def pair(p, first=False, last=False):
                    if not first:
                        copy_pT(2 * p - 1)
                    exponentials(2 * p, 0, 0, end=1)
                    if not first:
                        copy_o(2 * p - 1, 1)
                    exponentials(2 * p, 0, 0, start=1)
                    if not last:
                        relu_high(p + 1)
                    exponentials(2 * p, 0, 1)
                    copy_pT(2 * p)
                    exponentials(2 * p + 1, 1, 0)
                    if not last:
                        copy_q(p + 1)
                    exponentials(2 * p + 1, 1, 1)
                    copy_o(2 * p, 0)

                relu_high(0)
                copy_q(0)
                pair(0, first=True)
                with act.Fori(1, PAIRS - 1) as p:
                    pair(p)
                pair(PAIRS - 1, last=True)
                copy_pT(2 * PAIRS - 1)
                copy_o(2 * PAIRS - 1, 1)

            @block.gpsimd
            def _(pool):
                def add_bias(p):
                    pool.wait_ge(xn_ready, p + 1)
                    nc.gpsimd.tensor_tensor(x_pair(p), x_pair(p), rows[:, 2:3, :].to_broadcast([128, 2, D]),
                                            ALU.add).then_inc(bias_done, 1)

                def divide(t, g, half):
                    pool.wait_ge(rinv_ready, 2 * t + half + 1)
                    heads = slice(4 * half, 4 * half + 4)
                    nc.gpsimd.tensor_tensor(prob[g][:, heads, :], prob[g][:, heads, :],
                                            rinv[g][:, heads].unsqueeze(2).to_broadcast([128, 4, N]),
                                            ALU.mult).then_inc(prob_ready, 1)

                def pair(p, norms=True):
                    add_bias(p)
                    divide(2 * p, 0, 0)
                    divide(2 * p, 0, 1)
                    divide(2 * p + 1, 1, 0)
                    if norms:
                        inverse_root(pool, p + 2, stats_ready, rstd_ready)
                    divide(2 * p + 1, 1, 1)

                inverse_root(pool, 0, stats_ready, rstd_ready)
                inverse_root(pool, 1, stats_ready, rstd_ready)
                with pool.Fori(0, PAIRS - 2) as p:
                    pair(p)
                pair(PAIRS - 2, norms=False)
                pair(PAIRS - 1, norms=False)

            @block.vector
            def _(dve):
                def normalise(p):
                    dve.wait_ge(rstd_ready, p + 1)
                    dve.wait_ge(tr_done, since(p))
                    for g in range(2):
                        ins = nc.vector.tensor_scalar(xn[:, g, :], x_of(p, g), mv[:, 0, g, 0:1], rstd[:, 0, g:g + 1],
                                                      ALU.subtract, ALU.mult)
                    ins.then_inc(xn_ready, 1)

                def copy_k(p):
                    dve.wait_ge(k_done, p + 1)
                    for c in range(C):
                        ins = nc.vector.tensor_scalar(kT[:, c, :, :].rearrange("p g n -> p (g n)"), KY[:, c * 2 * N:(c + 1) * 2 * N],
                                                      bk[:, c:c + 1], None, ALU.add)
                    ins.then_inc(k_ready, 1)

                def copy_v(t, g):
                    dve.wait_ge(v_done, t + 1)
                    nc.vector.tensor_tensor(val[:, g, 0:D], VV[:, 0:D], rows[:, 1, :], ALU.add).then_inc(v_ready, 1)

                def mask_max(t, g):
                    for half in range(2):
                        for r in range(2 * half, 2 * half + 2):
                            dve.wait_ge(s_done, R * t + r + 1)
                            nc.vector.tensor_tensor(wide[g][:, r * C:(r + 1) * C, :],
                                                    SS[r][:, 0:C * N].rearrange("p (c n) -> p c n", c=C),
                                                    mbias_pair, ALU.add).then_inc(s_masked, 1)
                        dve.wait_ge(s_masked, R * t + 2 * half + 2)
                        nc.vector.tensor_reduce(nmax[g][:, 4 * half:4 * half + 4], wide[g][:, 4 * half:4 * half + 4, :],
                                                AX_X, ALU.max, negate=True).then_inc(nmax_ready, 1)

                def inverse(t, g, half):
                    dve.wait_ge(exp_done, 2 * t + half + 1)
                    nc.vector.reciprocal(rinv[g][:, 4 * half:4 * half + 4],
                                         rsum[g][:, 4 * half:4 * half + 4]).then_inc(rinv_ready, 1)

                def low_h(p):
                    dve.wait_ge(high_ready, p + 1)
                    nc.vector.scalar_tensor_tensor(hT_low, TQ[:, :], 0.0, hT_high.bitcast(F32), ALU.max,
                                                   ALU.subtract).then_inc(low_ready, 1)

                def low_o(t, g):
                    dve.wait_ge(o_high_ready, t + 1)
                    nc.vector.tensor_tensor(oTs[1][:, g, :, :], OT[:, 0:D].rearrange("p (c n) -> p c n", c=C),
                                            oTs[0][:, g, :, :].bitcast(F32), ALU.subtract).then_inc(o_ready, 1)

                def update(p):
                    dve.wait_ge(y_done, p + 1)
                    dve.wait_ge(bias_done, p + 1)
                    nc.vector.tensor_tensor(x_pair(p), KY[:, :].rearrange("p (g d) -> p g d", g=2), x_pair(p),
                                            ALU.add).then_inc(x_done, 1)

                def pair(p, first=False, last=False, norms=True):
                    mask_max(2 * p, 0)
                    if not first:
                        low_o(2 * p - 1, 1)
                    copy_v(2 * p + 1, 1)
                    inverse(2 * p, 0, 0)
                    if not last:
                        low_h(p + 1)
                    if not first:
                        update(p - 1)
                    inverse(2 * p, 0, 1)
                    mask_max(2 * p + 1, 1)
                    if norms:
                        layer_norm_stats(dve, p + 2, dstep, stats_ready)
                    inverse(2 * p + 1, 1, 0)
                    if not last:
                        copy_k(p + 1)
                    if norms:
                        normalise(p + 2)
                    inverse(2 * p + 1, 1, 1)
                    low_o(2 * p, 0)
                    if not last:
                        copy_v(2 * p + 2, 0)

                layer_norm_stats(dve, 0, dstep, stats_ready)
                normalise(0)
                low_h(0)
                layer_norm_stats(dve, 1, dstep, stats_ready)
                normalise(1)
                copy_k(0)
                copy_v(0, 0)
                pair(0, first=True)
                with dve.Fori(1, PAIRS - 2) as p:
                    pair(p)
                pair(PAIRS - 2, norms=False)
                pair(PAIRS - 1, last=True, norms=False)
                low_o(2 * PAIRS - 1, 1)
                update(PAIRS - 1)

            @block.sync
            def _(sp):
                with sp.Fori(0, PAIRS) as p:
                    sp.wait_ge(x_done, 1)
                    sp.wait_ge(x_done, p + 1)
                    sp.dma_start(out[bass.ds(2 * p, 2), :, :].rearrange("g n d -> n g d"), x_pair(p)).then_inc(stored, 16)
                sp.wait_ge(stored, 16 * PAIRS)


_INS = ["x", "adj", "L0_gnn_Wq", "L0_gnn_Wk", "L0_gnn_Wv", "L1_gnn_W", "L1_gnn_a", "L1_gnn_beta", "L2_gnn_weight",
        "L2_gnn_bias", "L3_gnn_Wq", "L3_gnn_bq", "L3_gnn_Wk", "L3_gnn_bk", "L3_gnn_Wv", "L3_gnn_bv", "L3_gnn_Wo", "L3_gnn_bo"]


def kernel(**inputs):
    import numpy as _np
    import concourse.bacc as _bacc
    from concourse import mybir as _mybir
    from concourse.bass_utils import run_bass_kernel_spmd as _run

    nc = _bacc.Bacc("TRN2", target_bir_lowering=False, num_devices=1)
    arrays, aps = {}, {}
    for name in _INS:
        a = _np.ascontiguousarray(inputs[name])
        arrays[f"in_{name}_dram"] = a
        aps[name] = nc.dram_tensor(f"in_{name}_dram", a.shape, _mybir.dt.from_np(a.dtype), kind="ExternalInput").ap()
    aps["out"] = nc.dram_tensor("out_0_dram", inputs["x"].shape, _mybir.dt.from_np(_np.dtype("float32")),
                                kind="ExternalOutput").ap()
    gnn_stack_kernel(nc, aps["x"], aps["adj"], aps)
    r = _run(nc, [arrays], core_ids=[0])
    return r.results[0]["out_0_dram"]
```

```python
from contextlib import ExitStack

import numpy as np

import concourse.bass as bass
from concourse import mybir

F32 = mybir.dt.float32
F32R = mybir.dt.float32r
ALU = mybir.AluOpType
ACT = mybir.ActivationFunctionType
AX_X = mybir.AxisListType.X


def gnn_stack_kernel(nc, x, adj, w):
    GRAPHS, N, D = x.shape
    PAIRS = GRAPHS // 2
    C = D // 128
    HEADS = 8
    HD = D // HEADS
    R = 128 // HD
    EPS = 1e-5
    ALPHA = 0.2
    QSCALE = float(HD) ** -0.5
    out = w["out"]
    assert N == 128 and C == 2 and HD == 32 and GRAPHS % 2 == 0

    with ExitStack() as ctx:
        def sb(name, shape, dt=F32):
            return ctx.enter_context(nc.sbuf_tensor(name, shape, dt))

        def sem(name):
            return ctx.enter_context(nc.semaphore(name))

        bank = [ctx.enter_context(nc.psum_tensor(f"bank{i}", [128, 512], F32)) for i in range(8)]

        xs = sb("xs", [128, GRAPHS, D])
        ident = sb("ident", [128, 128])
        ones = sb("ones", [128, 128])
        adj_sb = sb("adj_sb", [128, N])
        m_qk = [sb(f"m_qk{k}", [128, C, D], F32R) for k in range(2)]
        wv0T = [sb(f"wv0T{k}", [128, C, D], F32R) for k in range(2)]
        w1 = sb("w1", [128, C, D + 1])
        wa2 = sb("wa2", [128, C, N])
        beta = sb("beta", [128, 1])
        nadjT = sb("nadjT", [128, N])
        w2 = [sb(f"w2_{k}", [128, C, D], F32R) for k in range(2)]
        rows = sb("rows", [128, 3, D])
        mbias = sb("mbias", [128, N])
        wq3 = [sb(f"wq3_{k}", [128, C, D], F32R) for k in range(2)]
        wk3 = [sb(f"wk3_{k}", [128, C, D], F32R) for k in range(2)]
        wv3 = [sb(f"wv3_{k}", [128, C, D], F32R) for k in range(2)]
        wo3 = [sb(f"wo3_{k}", [128, C, D], F32R) for k in range(2)]
        bq = sb("bq", [128, C])
        bk = sb("bk", [128, C])
        mhalf = sb("mhalf", [128, 2])
        stats = sb("stats", [128, 2, 2, 6])
        mv = sb("mv", [128, 2, 2, 2])
        vare = sb("vare", [128, 2, 2])
        nmean = sb("nmean", [128, 2, 2])
        rstd = sb("rstd", [128, 2, 2])
        shift = sb("shift", [128, 2, 2])
        xn = sb("xn", [128, 2, D])
        xn2 = sb("xn2", [128, 2, D])
        hT = sb("hT", [128, C, 2, N])
        hTs = [sb(f"hTs{k}", [128, C, 2, N], F32R) for k in range(2)]
        yTs = [[sb(f"yTs{b}{k}", [128, C, 2, N], F32R) for k in range(2)] for b in range(2)]
        tT = sb("tT", [128, C, 2, N])
        val = sb("val", [128, 2, D + 1])
        val1 = sb("val1", [128, 2, D + 1])
        relm = sb("relm", [128, 2, N])
        oTs = [sb(f"oTs{k}", [128, 2, C, N], F32R) for k in range(2)]
        relsq = sb("relsq", [128, 2, N])
        rels = [sb(f"rels{k}", [128, 2, N], F32R) for k in range(2)]
        vals = [oTs[k][:, :, :, :].rearrange("p g c n -> p g (c n)") for k in range(2)]
        norm2 = sb("norm2", [128, 2])
        rnorm = sb("rnorm", [128, 2])
        wide = [sb(f"wide{g}", [128, HEADS, N]) for g in range(2)]
        prob = [sb(f"prob{g}", [128, HEADS, N]) for g in range(2)]
        probT = sb("probT", [128, HEADS, N])
        qT = sb("qT", [128, C, 2, N])
        kT = sb("kT", [128, C, 2, N])
        small = sb("small", [128, 64])
        adj_pair = adj_sb[:, :].unsqueeze(1).to_broadcast([128, 2, N])
        mbias_pair = mbias[:, :].unsqueeze(1).to_broadcast([128, 2, N])

        def x_of(p, g):
            return xs[:, bass.ds(2 * p + g, 1), :].rearrange("p a d -> p (a d)")

        def x_pair(p):
            return xs[:, bass.ds(2 * p, 2), :]

        def since(n):
            return max(n, 0) if isinstance(n, int) else n

        def moments(dve, p, dve_step, b=0):
            for g in range(2):
                ins = nc.vector.bn_stats(stats[:, b, g, :], x_of(p, g))
            ins.then_inc(dve_step, 1)

        def mean_variance(dve, p, dve_step, b=0):
            dve.wait_ge(dve_step, 1)
            dve.wait_ge(dve_step, 2 * p + 1)
            for g in range(2):
                ins = nc.vector.bn_aggr(mv[:, b, g, :], stats[:, b, g, :])
            ins.then_inc(dve_step, 1)

        def root_argument(dve, p, dve_step, stats_ready, b=0):
            dve.wait_ge(dve_step, 2 * p + 2)
            nc.vector.tensor_scalar(nmean[:, b, :], mv[:, b, :, 0], -1.0, None, ALU.mult)
            nc.vector.tensor_scalar(vare[:, b, :], mv[:, b, :, 1], EPS, None, ALU.add).then_inc(stats_ready, 1)

        def layer_norm_stats(dve, p, dve_step, stats_ready, b=0):
            moments(dve, p, dve_step, b)
            mean_variance(dve, p, dve_step, b)
            root_argument(dve, p, dve_step, stats_ready, b)

        def inverse_root(pool, p, stats_ready, rstd_ready, b=0):
            pool.wait_ge(stats_ready, p + 1)
            nc.gpsimd.tensor_tensor(rstd[:, b, :], vare[:, b, :], mhalf[:, :], ALU.pow).then_inc(rstd_ready, 1)

        def root_and_shift(pool, p, stats_ready, rstd_ready, shift_ready, b=0):
            inverse_root(pool, p, stats_ready, rstd_ready, b)
            pool.wait_ge(rstd_ready, p + 1)
            nc.gpsimd.tensor_tensor(shift[:, b, :], nmean[:, b, :], rstd[:, b, :], ALU.mult).then_inc(shift_ready, 1)

        def transposes(pe_ps):
            for c in range(C):
                for g in range(2):
                    ins = nc.tensor.transpose(pe_ps[:, c * 2 * N + g * N:c * 2 * N + (g + 1) * N],
                                              xn[:, g, c * 128:(c + 1) * 128], ident[:, :])
            return ins

        hT_high = hTs[0][:, :, :, :].rearrange("p c g n -> p (c g n)")
        hT_low = hTs[1][:, :, :, :].rearrange("p c g n -> p (c g n)")
        hT_flat = hT[:, :, :, :].rearrange("p c g n -> p (c g n)")

        x_first, x_second, x_loaded = sem("l0_x_first"), sem("l0_x_second"), sem("l0_x_loaded")
        xn_ready, tr_done, hT_ready = sem("l0_xn_ready"), sem("l0_tr_done"), sem("l0_hT_ready")
        t_done, tT_ready, v_done, v_ready = sem("l0_t_done"), sem("l0_tT_ready"), sem("l0_v_done"), sem("l0_v_ready")
        rel_done, relm_ready, relsq_ready = sem("l0_rel_done"), sem("l0_relm_ready"), sem("l0_relsq_ready")
        n2_ready, rn_ready = sem("l0_norm2_ready"), sem("l0_rnorm_ready")
        high_ready, low_ready = sem("l0_high_ready"), sem("l0_low_ready")
        stats_ready, rstd_ready = sem("l0_stats_ready"), sem("l0_rstd_ready")
        out_done, x_done, dstep = sem("l0_out_done"), sem("l0_x_done"), sem("l0_dve_step")
        l0_x_done = x_done
        w_high, v_high, relm_high, relm_low = sem("l0_w_high"), sem("l0_v_high"), sem("l0_relm_high"), sem("l0_relm_low")
        qk_loaded, v1_loaded, adj_loaded = sem("c_qk_loaded"), sem("c_v1_loaded"), sem("c_adj_loaded")
        rows_loaded = sem("c_rows_loaded")
        raw_loaded = [sem(f"c_raw_loaded{k}") for k in range(5)]
        c_zeros, c_ident, c_ones, c_mhalf = sem("c_zeros"), sem("c_ident"), sem("c_ones"), sem("c_mhalf")
        m_done, turned, wa_done, adjT_done = sem("c_m_done"), sem("c_turned"), sem("c_wa_done"), sem("c_adjT_done")
        c_high, c_low = sem("c_high"), sem("c_low")
        w1T_ready, deg_step, deg_root, adjn_ready = sem("c_w1T_ready"), sem("c_deg_step"), sem("c_deg_root"), sem("c_adjn_ready")
        FIRST = 4
        HT, MM, WV, W1, WA, AT = bank[0], bank[7], bank[3], bank[4], bank[5], bank[6]
        raw = [sb(f"raw{k}", [128, C, D]) for k in range(5)]
        with ExitStack() as cctx:
            def tmp(name, shape):
                return cctx.enter_context(nc.sbuf_tensor(name, shape, F32))

            wq0, wk0, wv0, w1T = (tmp(name, [128, C, D]) for name in ("wq0", "wk0", "wv0", "w1T"))
            a12 = tmp("a12", [128, 2, C])
            deg = tmp("deg", [128, 6])
            adjn = tmp("adjn", [128, N])
            def chunks(weight):
                return weight.rearrange("(c p) n -> p c n", p=128)

            def as_chunks(ps):
                return ps[:, :].rearrange("p (c n) -> p c n", c=C)

            with nc.Block() as block:
                @block.sync
                def _(sp):
                    sp.dma_start(wq0[:, :, :], chunks(w["L0_gnn_Wq"])).then_inc(qk_loaded, 16)
                    sp.dma_start(wk0[:, :, :], chunks(w["L0_gnn_Wk"])).then_inc(qk_loaded, 16)
                    sp.dma_start(adj_sb[:, :], adj).then_inc(adj_loaded, 16)
                    sp.dma_start(wv0[:, :, :], chunks(w["L0_gnn_Wv"])).then_inc(v1_loaded, 16)
                    sp.dma_start(w1[:, :, 0:D], chunks(w["L1_gnn_W"])).then_inc(v1_loaded, 16)
                    with nc.allow_non_contiguous_dma("columns of small vectors"):
                        sp.dma_start(a12[:, :, :].rearrange("p k c -> p (k c)"),
                                     w["L1_gnn_a"].rearrange("(k p) o -> p (k o)", p=128)).then_inc(v1_loaded, 16)
                    for k, name in enumerate(("L2_gnn_weight", "L3_gnn_Wq", "L3_gnn_Wk", "L3_gnn_Wv", "L3_gnn_Wo")):
                        sp.dma_start(raw[k][:, :, :], chunks(w[name])).then_inc(raw_loaded[k], 16)

                @block.gpsimd
                def _(pool):
                    nc.gpsimd.memset(mhalf[:, :], -0.5).then_inc(c_mhalf, 1)
                    nc.gpsimd.memset(ident[:, :], 0.0).then_inc(c_zeros, 1)
                    nc.gpsimd.memset(ones[:, :], 1.0).then_inc(c_ones, 1)
                    pool.wait_ge(c_zeros, 1)
                    nc.gpsimd.affine_select(out=ident[:, :], in_=ident[:, :], compare_op=ALU.not_equal, fill=1.0,
                                            base=0, pattern=[[-1, 128]], channel_multiplier=1).then_inc(c_ident, 1)
                    pool.wait_ge(c_mhalf, 1)
                    inverse_root(pool, 0, stats_ready, rstd_ready)
                    pool.wait_ge(deg_step, 2)
                    nc.gpsimd.tensor_tensor(deg[:, 4:5], deg[:, 2:3], mhalf[:, 0:1], ALU.pow).then_inc(deg_root, 1)
                    inverse_root(pool, 1, stats_ready, rstd_ready)
                    inverse_root(pool, 2, stats_ready, rstd_ready)

                @block.tensor
                def _(pe):
                    pe.wait_ge(qk_loaded, 32)
                    for d in range(C):
                        for e in range(C):
                            ins = nc.tensor.matmul(MM[:, d * D:(d + 1) * D], wq0[:, e, d * 128:(d + 1) * 128],
                                                   wk0[:, e, :], start=(e == 0), stop=(e == C - 1))
                    ins.then_inc(m_done, 1)
                    pe.wait_ge(c_ident, 1)
                    pe.wait_ge(xn_ready, 1)
                    transposes(HT).then_inc(tr_done, 1)
                    pe.wait_ge(v1_loaded, 48)
                    for ps, src in ((WV, wv0), (W1, w1)):
                        for c in range(C):
                            for e in range(C):
                                ins = nc.tensor.transpose(ps[:, c * D + e * 128:c * D + (e + 1) * 128],
                                                          src[:, e, c * 128:(c + 1) * 128], ident[:, :])
                        ins.then_inc(turned, 1)
                    pe.wait_ge(adjn_ready, 1)
                    nc.tensor.transpose(AT[:, 0:N], adjn[:, :], ident[:, :]).then_inc(adjT_done, 1)
                    pe.wait_ge(w1T_ready, 1)
                    for c in range(C):
                        for f in range(C):
                            ins = nc.tensor.matmul(WA[:, 2 * c:2 * c + 2], w1T[:, f, c * 128:(c + 1) * 128],
                                                   a12[:, :, f], start=(f == 0), stop=(f == C - 1))
                    ins.then_inc(wa_done, 1)

                @block.vector
                def _(dve):
                    dve.wait_ge(x_first, 16)
                    layer_norm_stats(dve, 0, dstep, stats_ready)
                    dve.wait_ge(rstd_ready, 1)
                    for g in range(2):
                        ins = nc.vector.tensor_scalar(xn[:, g, :], xs[:, g, :], mv[:, 0, g, 0:1], rstd[:, 0, g:g + 1],
                                                      ALU.subtract, ALU.mult)
                    ins.then_inc(xn_ready, 1)
                    dve.wait_ge(adj_loaded, 16)
                    nc.vector.tensor_reduce(deg[:, 0:1], adj_sb[:, :], AX_X, ALU.add).then_inc(deg_step, 1)
                    dve.wait_ge(deg_step, 1)
                    nc.vector.tensor_scalar(deg[:, 1:2], deg[:, 0:1], 0.0, None, ALU.is_gt)
                    nc.vector.tensor_scalar(deg[:, 2:3], deg[:, 0:1], float(np.finfo(np.float32).tiny), None,
                                            ALU.max).then_inc(deg_step, 1)
                    dve.wait_ge(c_high, 1)
                    nc.vector.tensor_tensor(m_qk[1][:, :, :], as_chunks(MM), m_qk[0][:, :, :].bitcast(F32), ALU.subtract)
                    dve.wait_ge(high_ready, 1)
                    nc.vector.scalar_tensor_tensor(hT_low, HT[:, :], 0.0, hT_high.bitcast(F32), ALU.max,
                                                   ALU.subtract).then_inc(low_ready, 1)
                    dve.wait_ge(x_second, 16)
                    layer_norm_stats(dve, 1, dstep, stats_ready)
                    dve.wait_ge(deg_root, 1)
                    nc.vector.tensor_tensor(deg[:, 3:4], deg[:, 1:2], deg[:, 4:5], ALU.mult).then_inc(deg_step, 1)
                    nc.vector.tensor_scalar(mbias[:, :], adj_sb[:, :], -1.0, 1e9, ALU.add, ALU.mult)
                    dve.wait_ge(deg_step, 3)
                    nc.vector.tensor_scalar(adjn[:, :], adj_sb[:, :], deg[:, 3:4], None, ALU.mult).then_inc(adjn_ready, 1)
                    dve.wait_ge(turned, 2)
                    nc.vector.tensor_copy(w1T[:, :, :], as_chunks(W1)).then_inc(w1T_ready, 1)
                    dve.wait_ge(c_high, 2)
                    nc.vector.tensor_tensor(wv0T[1][:, :, :], as_chunks(WV), wv0T[0][:, :, :].bitcast(F32), ALU.subtract)
                    dve.wait_ge(rstd_ready, 2)
                    for g in range(2):
                        ins = nc.vector.tensor_scalar(xn[:, g, :], xs[:, 2 + g, :], mv[:, 0, g, 0:1], rstd[:, 0, g:g + 1],
                                                      ALU.subtract, ALU.mult)
                    ins.then_inc(xn_ready, 1)
                    layer_norm_stats(dve, 2, dstep, stats_ready)
                    dve.wait_ge(adjT_done, 1)
                    nc.vector.tensor_scalar(nadjT[:, :], AT[:, 0:N], deg[:, 3:4], None, ALU.mult)
                    dve.wait_ge(rows_loaded, 96)
                    nc.vector.tensor_scalar(bq[:, :], bq[:, :], QSCALE, None, ALU.mult)
                    dve.wait_ge(c_ones, 1)
                    dve.wait_ge(wa_done, 1)
                    nc.vector.tensor_copy(w1[:, :, D:D + 1], WA[:, 0:2 * C:2].unsqueeze(2))
                    for c in range(C):
                        ins = nc.vector.tensor_scalar(wa2[:, c, :], ones[:, :], WA[:, 2 * c + 1:2 * c + 2], None, ALU.mult)
                    ins.then_inc(c_low, 1)
                    dve.wait_ge(c_low, 1)

                @block.scalar
                def _(act):
                    act.dma_start(xs[:, 0:2, :], x[0:2, :, :].rearrange("g n d -> n g d")).then_inc(x_first, 16)
                    act.dma_start(xs[:, 2:2 * FIRST, :], x[2:2 * FIRST, :, :].rearrange("g n d -> n g d")).then_inc(x_second, 16)
                    for k, name in enumerate(("L2_gnn_bias", "L3_gnn_bv", "L3_gnn_bo")):
                        act.dma_start(rows[:, k, :], w[name].rearrange("(o n) -> o n", o=1).to_broadcast([128, D])).then_inc(rows_loaded, 16)
                    act.dma_start(beta[:, :], w["L1_gnn_beta"].rearrange("(o n) -> o n", o=1).to_broadcast([128, 1])).then_inc(rows_loaded, 16)
                    with nc.allow_non_contiguous_dma("columns of small vectors"):
                        act.dma_start(bq[:, :], w["L3_gnn_bq"].rearrange("(c p) -> p c", p=128)).then_inc(rows_loaded, 16)
                        act.dma_start(bk[:, :], w["L3_gnn_bk"].rearrange("(c p) -> p c", p=128)).then_inc(rows_loaded, 16)
                    act.wait_ge(m_done, 1)
                    nc.scalar.copy(m_qk[0][:, :, :], as_chunks(MM)).then_inc(c_high, 1)
                    act.wait_ge(tr_done, 1)
                    nc.scalar.activation(hT_high, HT[:, :], ACT.Relu).then_inc(high_ready, 1)
                    act.wait_ge(turned, 1)
                    nc.scalar.copy(wv0T[0][:, :, :], as_chunks(WV)).then_inc(c_high, 1)
                    act.wait_ge(low_ready, 1)
                    nc.scalar.activation(hT_flat, HT[:, :], ACT.Relu).then_inc(hT_ready, 1)

        l1_stats_ready, l1_rstd_ready, l1_shift_ready = sem("l1_stats_ready"), sem("l1_rstd_ready"), sem("l1_shift_ready")
        l1_xn_ready, l1_tr_done, l1_hT_ready, l1_step = sem("l1_xn_ready"), sem("l1_tr_done"), sem("l1_hT_ready"), sem("l1_dve_step")
        l2_stats_ready, l2_rstd_ready, l2_shift_ready = sem("l2_stats_ready"), sem("l2_rstd_ready"), sem("l2_shift_ready")
        l2_xn_ready, l2_yt_done, l2_step = sem("l2_xn_ready"), sem("l2_yt_done"), sem("l2_dve_step")
        l2_high_ready, l2_yt_ready = sem("l2_high_ready"), sem("l2_yt_ready")
        yT_high = [yTs[b][0][:, :, :, :].rearrange("p c g n -> p (c g n)") for b in range(2)]
        yT_low = [yTs[b][1][:, :, :, :].rearrange("p c g n -> p (c g n)") for b in range(2)]
        l3_stats_ready, l3_rstd_ready, l3_step = sem("l3_stats_ready"), sem("l3_rstd_ready"), sem("l3_dve_step")
        l3_xn_ready, l3_tr_done, l3_high_ready, l3_low_ready = sem("l3_xn_ready"), sem("l3_tr_done"), sem("l3_high_ready"), sem("l3_low_ready")

        def relu_norm(act, p, b, dst, shift_ready):
            act.wait_ge(shift_ready, p + 1)
            for g in range(2):
                ins = nc.scalar.activation(dst[:, g, :], x_of(p, g), ACT.Relu, bias=shift[:, b, g:g + 1],
                                           scale=rstd[:, b, g:g + 1])
            return ins

        def gather_nodes(pe, ps, p, src, xn_ready):
            pe.wait_ge(xn_ready, p + 1)
            for c in range(C):
                for g in range(2):
                    ins = nc.tensor.matmul(ps[:, (2 * c + g) * N:(2 * c + g + 1) * N],
                                           src[:, g, c * 128:(c + 1) * 128], nadjT[:, :], start=True, stop=True)
            return ins


        def node_product(ps_g, weight, g):
            for c in range(C):
                ins = nc.tensor.matmul(ps_g, hT[:, c, g, :], weight[:, c, :], start=(c == 0), stop=(c == C - 1))
            return ins

        PARTS = ((0, 0), (0, 1), (1, 0))

        def split_product(ps, lhsT, rhs):
            terms = [(a, b, c) for c in range(C) for a, b in PARTS]
            for n, (a, b, c) in enumerate(terms):
                ins = nc.tensor.matmul(ps, lhsT(a, c), rhs(b, c), start=(n == 0), stop=(n == len(terms) - 1))
            return ins

        def node_split_product(ps_g, weight, g):
            return split_product(ps_g, lambda k, c: hTs[k][:, c, g, :], lambda k, c: weight[k][:, c, :])

        def feature_product(ps, weight):
            for m in range(C):
                ins = split_product(ps[:, m * 2 * N:(m + 1) * 2 * N],
                                    lambda k, c: weight[k][:, c, m * 128:(m + 1) * 128],
                                    lambda k, c: hTs[k][:, c, :, :].rearrange("p g n -> p (g n)"))
            return ins

        HT, TT, VV, RR, NO, OO = bank[0:6]

        with nc.Block() as block:
            @block.sync
            def _(sp):
                sp.dma_start(xs[:, 2 * FIRST:2 * FIRST + 2, :],
                             x[2 * FIRST:2 * FIRST + 2, :, :].rearrange("g n d -> n g d")).then_inc(x_loaded, 16)
                with sp.Fori(FIRST + 1, PAIRS) as p:
                    sp.wait_ge(x_loaded, 16 * (p - FIRST))
                    sp.dma_start(x_pair(p), x[bass.ds(2 * p, 2), :, :].rearrange("g n d -> n g d")).then_inc(x_loaded, 16)

            @block.tensor
            def _(pe):
                def turn(p):
                    pe.wait_ge(xn_ready, p + 1)
                    pe.wait_ge(hT_ready, since(p))
                    transposes(HT).then_inc(tr_done, 1)

                def t_product(p):
                    pe.wait_ge(low_ready, p + 1)
                    feature_product(TT, m_qk).then_inc(t_done, 1)

                def values(p):
                    pe.wait_ge(v_ready, since(p))
                    for g in range(2):
                        ins = node_split_product(VV[:, g * D:(g + 1) * D], wv0T, g)
                    ins.then_inc(v_done, 1)

                def relation(p):
                    pe.wait_ge(tT_ready, p + 1)
                    pe.wait_ge(hT_ready, p + 1)
                    pe.wait_ge(relm_ready, since(p))
                    for g in range(2):
                        for c in range(C):
                            ins = nc.tensor.matmul(RR[:, g * N:(g + 1) * N], hT[:, c, g, :], tT[:, c, g, :],
                                                   start=(c == 0), stop=(c == C - 1))
                    ins.then_inc(rel_done, 1)

                def outputs(p):
                    pe.wait_ge(relsq_ready, p + 1)
                    pe.wait_ge(x_done, since(p))
                    for g in range(2):
                        nc.tensor.matmul(NO[:, g:g + 1], relsq[:, g, :], ones[:, 0:1], start=True, stop=True)
                    pe.wait_ge(v_ready, p + 1)
                    pe.wait_ge(relm_low, p + 1)
                    for g in range(2):
                        for n, (a, b) in enumerate(PARTS):
                            ins = nc.tensor.matmul(OO[:, g * D:(g + 1) * D], rels[a][:, g, :], vals[b][:, g, :],
                                                   start=(n == 0), stop=(n == len(PARTS) - 1))
                    ins.then_inc(out_done, 1)

                t_product(0)
                turn(1)
                values(0)
                relation(0)

                def step(p):
                    t_product(p)
                    turn(p + 1)
                    values(p)
                    relation(p)
                    outputs(p - 1)

                step(1)
                step(2)
                with pe.Fori(1, PAIRS // 2 - 1) as j:
                    step(2 * j + 1)
                    step(2 * j + 2)
                t_product(PAIRS - 1)
                values(PAIRS - 1)
                relation(PAIRS - 1)
                outputs(PAIRS - 2)
                pe.wait_ge(l1_xn_ready, 1)
                transposes(HT).then_inc(l1_tr_done, 1)
                outputs(PAIRS - 1)

            @block.scalar
            def _(act):
                def relu_high(p):
                    act.wait_ge(tr_done, p + 1)
                    act.wait_ge(v_done, since(p))
                    nc.scalar.activation(hT_high, HT[:, :], ACT.Relu).then_inc(high_ready, 1)

                def relu_T(p):
                    act.wait_ge(low_ready, p + 1)
                    act.wait_ge(rel_done, since(p))
                    nc.scalar.activation(hT_flat, HT[:, :], ACT.Relu).then_inc(hT_ready, 1)

                def copy_t(p):
                    act.wait_ge(t_done, p + 1)
                    nc.scalar.copy(tT[:, :, :, :].rearrange("p c g n -> p (c g n)"), TT[:, :]).then_inc(tT_ready, 1)

                def copy_v(p):
                    act.wait_ge(v_done, p + 1)
                    act.wait_ge(out_done, since(p))
                    nc.scalar.copy(vals[0][:, :, :], VV[:, :].rearrange("p (g n) -> p g n", g=2)).then_inc(v_high, 1)

                def relation_high(p):
                    act.wait_ge(relm_ready, p + 1)
                    act.wait_ge(out_done, since(p))
                    nc.scalar.copy(rels[0][:, :, :], relm[:, :, :]).then_inc(relm_high, 1)

                for k, parts in enumerate((w2, wq3, wk3, wv3, wo3)):
                    act.wait_ge(raw_loaded[k], 16)
                    nc.scalar.copy(parts[0][:, :, :], raw[k][:, :, :]).then_inc(w_high, 1)
                copy_t(0)
                relu_high(1)
                relu_T(1)
                copy_v(0)
                relation_high(0)

                def step(p):
                    copy_t(p)
                    relu_high(p + 1)
                    relu_T(p + 1)
                    copy_v(p)
                    relation_high(p)

                with act.Fori(0, PAIRS // 2 - 1) as j:
                    step(2 * j + 1)
                    step(2 * j + 2)
                copy_t(PAIRS - 1)
                act.wait_ge(tr_done, PAIRS)
                relu_norm(act, 0, 0, xn, l1_shift_ready).then_inc(l1_xn_ready, 1)
                copy_v(PAIRS - 1)
                relation_high(PAIRS - 1)
                act.wait_ge(l1_tr_done, 1)
                act.wait_ge(rel_done, PAIRS)
                nc.scalar.copy(hT_flat, HT[:, :]).then_inc(l1_hT_ready, 1)
                relu_norm(act, 1, 1, xn, l1_shift_ready).then_inc(l1_xn_ready, 1)

            @block.gpsimd
            def _(pool):
                def squares(p):
                    pool.wait_ge(relm_ready, p + 1)
                    pool.wait_ge(out_done, since(p))
                    nc.gpsimd.tensor_tensor(relsq[:, :, :], relm[:, :, :], relm[:, :, :], ALU.mult).then_inc(relsq_ready, 1)

                def relation_low(p):
                    pool.wait_ge(relm_high, p + 1)
                    nc.gpsimd.tensor_tensor(rels[1][:, :, :], relm[:, :, :], rels[0][:, :, :].bitcast(F32),
                                            ALU.subtract).then_inc(relm_low, 1)

                def inverse_norm(p):
                    pool.wait_ge(n2_ready, p + 1)
                    nc.gpsimd.tensor_tensor(rnorm[:, :], norm2[:, :], mhalf[:, :], ALU.pow).then_inc(rn_ready, 1)

                inverse_root(pool, 3, stats_ready, rstd_ready)
                squares(0)
                relation_low(0)

                def step(p):
                    squares(p)
                    inverse_norm(p - 1)
                    relation_low(p)
                    inverse_root(pool, p + 3, stats_ready, rstd_ready)

                with pool.Fori(0, PAIRS // 2 - 2) as j:
                    step(2 * j + 1)
                    step(2 * j + 2)
                for n, p in enumerate(range(PAIRS - 3, PAIRS)):
                    squares(p)
                    inverse_norm(p - 1)
                    relation_low(p)
                    root_and_shift(pool, n, l1_stats_ready, l1_rstd_ready, l1_shift_ready, n % 2)
                inverse_norm(PAIRS - 1)

            @block.vector
            def _(dve):
                def statistics(p):
                    if not isinstance(p, int):
                        dve.wait_ge(x_loaded, 16 * (p - FIRST) + 16)
                    layer_norm_stats(dve, p, dstep, stats_ready)

                def normalise(p):
                    dve.wait_ge(rstd_ready, p + 1)
                    dve.wait_ge(tr_done, since(p))
                    for g in range(2):
                        ins = nc.vector.tensor_scalar(xn[:, g, :], x_of(p, g), mv[:, 0, g, 0:1], rstd[:, 0, g:g + 1],
                                                      ALU.subtract, ALU.mult)
                    ins.then_inc(xn_ready, 1)

                def low_part(p):
                    dve.wait_ge(high_ready, p + 1)
                    nc.vector.scalar_tensor_tensor(hT_low, HT[:, :], 0.0, hT_high.bitcast(F32), ALU.max,
                                                   ALU.subtract).then_inc(low_ready, 1)

                def mask(p):
                    dve.wait_ge(rel_done, p + 1)
                    dve.wait_ge(relsq_ready, since(p))
                    dve.wait_ge(relm_low, since(p))
                    nc.vector.tensor_tensor(relm[:, :, :], RR[:, 0:2 * N].rearrange("p (g n) -> p g n", g=2),
                                            adj_pair, ALU.mult).then_inc(relm_ready, 1)

                def low_v(p):
                    dve.wait_ge(v_high, p + 1)
                    nc.vector.tensor_tensor(vals[1][:, :, :], VV[:, :].rearrange("p (g n) -> p g n", g=2),
                                            vals[0][:, :, :].bitcast(F32), ALU.subtract).then_inc(v_ready, 1)

                def copy_norm2(p):
                    dve.wait_ge(out_done, p + 1)
                    nc.vector.tensor_copy(norm2[:, :], NO[:, 0:2]).then_inc(n2_ready, 1)

                def update(p):
                    dve.wait_ge(rn_ready, p + 1)
                    for g in range(2):
                        ins = nc.vector.scalar_tensor_tensor(x_of(p, g), OO[:, g * D:(g + 1) * D], rnorm[:, g:g + 1],
                                                             x_of(p, g), ALU.mult, ALU.add)
                    ins.then_inc(x_done, 1)

                for k, parts in enumerate((w2, wq3, wk3, wv3, wo3)):
                    dve.wait_ge(w_high, k + 1)
                    nc.vector.tensor_tensor(parts[1][:, :, :], raw[k][:, :, :], parts[0][:, :, :].bitcast(F32), ALU.subtract)
                low_part(1)
                normalise(2)
                statistics(3)
                mask(0)
                low_v(0)

                def step(p):
                    low_part(p + 1)
                    mask(p)
                    normalise(p + 2)
                    low_v(p)
                    copy_norm2(p - 1)
                    statistics(p + 3)
                    update(p - 1)

                with dve.Fori(0, PAIRS // 2 - 2) as j:
                    step(2 * j + 1)
                    step(2 * j + 2)
                for n, p in enumerate(range(PAIRS - 3, PAIRS)):
                    if p + 1 < PAIRS:
                        low_part(p + 1)
                    mask(p)
                    if p + 2 < PAIRS:
                        normalise(p + 2)
                    copy_norm2(p - 1)
                    low_v(p)
                    if n < 2:
                        layer_norm_stats(dve, n, l1_step, l1_stats_ready, n % 2)
                    update(p - 1)
                dve.wait_ge(l1_xn_ready, 1)
                layer_norm_stats(dve, 2, l1_step, l1_stats_ready)
                copy_norm2(PAIRS - 1)
                update(PAIRS - 1)

            xn_ready, tr_done, hT_ready, dstep = l1_xn_ready, l1_tr_done, l1_hT_ready, l1_step
            h_done, val_ready, e_done = sem("l1_h_done"), sem("l1_val_ready"), sem("l1_e_done")
            e_ready, em_ready, nmax_ready = sem("l1_e_ready"), sem("l1_em_ready"), sem("l1_nmax_ready")
            prob_ready, pt_done, pt_ready, att_done = sem("l1_prob_ready"), sem("l1_pt_done"), sem("l1_pt_ready"), sem("l1_att_done")
            l1_pt_ready = pt_ready
            rinv_ready, bh_ready, u_ready, umin_ready = sem("l1_rinv_ready"), sem("l1_bh_ready"), sem("l1_u_ready"), sem("l1_umin_ready")
            eu_ready, elu_ready, x_done = sem("l1_eu_ready"), sem("l1_elu_ready"), sem("l1_x_done")
            l1_x_done = x_done
            leaky_ready = sem("l1_leaky_ready")
            stats_ready, rstd_ready, shift_ready = l1_stats_ready, l1_rstd_ready, l1_shift_ready
            HT, HG, PT, EE, UU = bank[0], (bank[1], bank[2]), bank[3], bank[4], bank[5]
            valb = [val, val1]
            bh = [wide[b][:, 0:4, :].rearrange("p a n -> p (a n)").rearrange("p (g d) -> p g d", g=2) for b in range(2)]
            u_sb = wide[0][:, 4:8, :].rearrange("p a n -> p (a n)")
            umin = wide[1][:, 4:8, :].rearrange("p a n -> p (a n)")
            eu = prob[0][:, 0:4, :].rearrange("p a n -> p (a n)")
            elu = prob[0][:, 4:8, :].rearrange("p a n -> p (a n)")
            e_sb, em, p1, p1T = (prob[1][:, 2 * k:2 * k + 2, :] for k in range(4))
            el = tT[:, 1, :, :]
            nmax, rsum, rinv = small[:, 0:2], small[:, 2:4], small[:, 4:6]

            @block.tensor
            def _(pe):
                def turn(p):
                    pe.wait_ge(xn_ready, p + 1)
                    transposes(HT).then_inc(tr_done, 1)

                def product(p):
                    pe.wait_ge(hT_ready, p + 1)
                    pe.wait_ge(val_ready, since(p))
                    for g in range(2):
                        ins = node_product(HG[g][:, 0:D + 1], w1, g)
                    ins.then_inc(h_done, 1)

                def turn_prob(p):
                    pe.wait_ge(prob_ready, p + 1)
                    pe.wait_ge(pt_ready, since(p))
                    for g in range(2):
                        ins = nc.tensor.transpose(PT[:, g * N:(g + 1) * N], p1[:, g, :], ident[:, :])
                    ins.then_inc(pt_done, 1)

                def spread(p):
                    pe.wait_ge(e_ready, since(p))
                    for c in range(C):
                        ins = nc.tensor.matmul(EE[:, 0:2 * N], wa2[:, c, :], hT[:, c, :, :].rearrange("p g n -> p (g n)"),
                                               start=(c == 0), stop=(c == C - 1))
                    ins.then_inc(e_done, 1)

                def attend(p, b):
                    pe.wait_ge(pt_ready, p + 1)
                    pe.wait_ge(u_ready, since(p))
                    for g in range(2):
                        ins = nc.tensor.matmul(UU[:, g * D:(g + 1) * D], p1T[:, g, :], valb[b][:, g, 0:D], start=True, stop=True)
                    ins.then_inc(att_done, 1)

                def step(p, b, first=False, last=False, before=None):
                    product(p)
                    if not first:
                        turn_prob(p - 1)
                    if before is not None:
                        pe.wait_ge(before, PAIRS)
                    spread(p)
                    if not last:
                        turn(p + 1)
                    else:
                        gather_nodes(pe, HT, 0, xn, l2_xn_ready).then_inc(l2_yt_done, 1)
                    if not first:
                        attend(p - 1, 1 - b)

                step(0, 0, first=True, before=l0_x_done)
                step(1, 1)
                with pe.Fori(0, PAIRS // 4 - 1) as j:
                    for i in range(4):
                        step(4 * j + 2 + i, i % 2)
                step(PAIRS - 2, 0)
                step(PAIRS - 1, 1, last=True)
                turn_prob(PAIRS - 1)
                pe.wait_ge(val_ready, PAIRS)
                gather_nodes(pe, HG[0], 1, xn2, l2_xn_ready).then_inc(l2_yt_done, 1)
                attend(PAIRS - 1, 1)

            @block.scalar
            def _(act):
                def normalise(p, b):
                    act.wait_ge(tr_done, since(p))
                    relu_norm(act, p, b, xn, shift_ready).then_inc(xn_ready, 1)

                def copy_hT(p):
                    act.wait_ge(tr_done, p + 1)
                    act.wait_ge(e_done, since(p))
                    nc.scalar.copy(hT_flat, HT[:, :]).then_inc(hT_ready, 1)

                def copy_h(p, b):
                    act.wait_ge(h_done, p + 1)
                    act.wait_ge(att_done, since(p - 1))
                    act.wait_ge(bh_ready, since(p - 1))
                    for g in range(2):
                        ins = nc.scalar.copy(valb[b][:, g, :], HG[g][:, 0:D + 1])
                    ins.then_inc(val_ready, 1)

                def add_s1(p, b):
                    act.wait_ge(e_done, p + 1)
                    act.wait_ge(leaky_ready, since(p))
                    act.wait_ge(val_ready, p + 1)
                    for g in range(2):
                        ins = nc.scalar.activation(e_sb[:, g, :], EE[:, g * N:(g + 1) * N], ACT.Identity,
                                                   bias=valb[b][:, g, D:D + 1])
                    ins.then_inc(e_ready, 1)

                def softmax_exp(p):
                    act.wait_ge(nmax_ready, p + 1)
                    act.wait_ge(pt_done, since(p))
                    act.wait_ge(rinv_ready, since(p))
                    for g in range(2):
                        ins = nc.scalar.activation(p1[:, g, :], em[:, g, :], ACT.Exp, bias=nmax[:, g:g + 1],
                                                   accum_out=rsum[:, g:g + 1])
                    ins.then_inc(prob_ready, 1)

                def elu_exp(p):
                    act.wait_ge(umin_ready, p + 1)
                    act.wait_ge(elu_ready, since(p))
                    nc.scalar.activation(eu, umin, ACT.Exp).then_inc(eu_ready, 1)

                def step(p, b, lag=2, last=False, norms=True):
                    copy_h(p, b)
                    if lag >= 2:
                        elu_exp(p - 2)
                    add_s1(p, b)
                    if not last:
                        copy_hT(p + 1)
                    if norms:
                        normalise(p + 2, b)
                    elif not last:
                        act.wait_ge(tr_done, PAIRS)
                        relu_norm(act, 0, 0, xn, l2_shift_ready).then_inc(l2_xn_ready, 1)
                    else:
                        relu_norm(act, 1, 1, xn2, l2_shift_ready).then_inc(l2_xn_ready, 1)
                    softmax_exp(p)

                step(0, 0, lag=0)
                step(1, 1, lag=1)
                step(2, 0)
                step(3, 1)
                with act.Fori(1, PAIRS // 4 - 1) as j:
                    for i in range(4):
                        step(4 * j + i, i % 2)
                step(PAIRS - 4, 0)
                step(PAIRS - 3, 1)
                step(PAIRS - 2, 0, norms=False)
                step(PAIRS - 1, 1, last=True, norms=False)
                elu_exp(PAIRS - 2)
                act.wait_ge(l2_yt_done, 1)
                nc.scalar.copy(yT_high[0], HT[:, :]).then_inc(l2_high_ready, 1)
                act.wait_ge(l2_yt_done, 2)
                nc.scalar.copy(yT_high[1], HG[0][:, :]).then_inc(l2_high_ready, 1)
                relu_norm(act, 2, 0, xn, l2_shift_ready).then_inc(l2_xn_ready, 1)
                elu_exp(PAIRS - 1)

            @block.gpsimd
            def _(pool):
                def beta_h(p, b):
                    pool.wait_ge(val_ready, p + 1)
                    pool.wait_ge(u_ready, since(p - 1))
                    nc.gpsimd.tensor_tensor(bh[b], valb[b][:, :, 0:D], beta[:, :].unsqueeze(2).to_broadcast([128, 2, D]), ALU.mult).then_inc(bh_ready, 1)

                def add(p):
                    pool.wait_ge(elu_ready, p + 1)
                    nc.gpsimd.tensor_tensor(x_pair(p), x_pair(p), elu.rearrange("p (g d) -> p g d", g=2),
                                            ALU.add).then_inc(x_done, 1)

                def step(p, b, lag=2, norms=True):
                    beta_h(p, b)
                    if norms:
                        root_and_shift(pool, p + 3, stats_ready, rstd_ready, shift_ready, 1 - b)
                    else:
                        root_and_shift(pool, p + 3 - PAIRS, l2_stats_ready, l2_rstd_ready, l2_shift_ready, 1 - b)
                    if lag >= 2:
                        add(p - 2)

                step(0, 0, lag=0)
                step(1, 1, lag=1)
                step(2, 0)
                step(3, 1)
                with pool.Fori(1, PAIRS // 4 - 1) as j:
                    for i in range(4):
                        step(4 * j + i, i % 2)
                for p in range(PAIRS - 4, PAIRS):
                    step(p, p % 2, norms=p + 3 < PAIRS)
                add(PAIRS - 2)
                add(PAIRS - 1)

            @block.vector
            def _(dve):
                def copy_pT(p):
                    dve.wait_ge(pt_done, p + 1)
                    dve.wait_ge(att_done, since(p))
                    nc.vector.tensor_copy(p1T, PT[:, 0:2 * N].rearrange("p (g n) -> p g n", g=2)).then_inc(pt_ready, 1)
                    nc.vector.reciprocal(rinv, rsum).then_inc(rinv_ready, 1)

                def elu_max(p):
                    dve.wait_ge(eu_ready, p + 1)
                    dve.wait_ge(x_done, since(p))
                    nc.vector.scalar_tensor_tensor(elu, eu, -1.0, u_sb, ALU.add, ALU.max).then_inc(elu_ready, 1)

                def leaky(p):
                    dve.wait_ge(e_ready, p + 1)
                    nc.vector.scalar_tensor_tensor(el, e_sb, ALPHA, e_sb, ALU.mult, ALU.max).then_inc(leaky_ready, 1)

                def mask(p):
                    dve.wait_ge(leaky_ready, p + 1)
                    dve.wait_ge(prob_ready, since(p))
                    nc.vector.tensor_tensor(em, el, adj_pair, ALU.mult).then_inc(em_ready, 1)

                def maximum(p):
                    dve.wait_ge(em_ready, p + 1)
                    nc.vector.tensor_reduce(nmax, em, AX_X, ALU.max, negate=True).then_inc(nmax_ready, 1)

                def gather(p, b):
                    dve.wait_ge(att_done, p + 1)
                    dve.wait_ge(bh_ready, p + 1)
                    dve.wait_ge(rinv_ready, p + 1)
                    dve.wait_ge(elu_ready, since(p))
                    for g in range(2):
                        ins = nc.vector.scalar_tensor_tensor(u_sb[:, g * D:(g + 1) * D], UU[:, g * D:(g + 1) * D],
                                                             rinv[:, g:g + 1], bh[b][:, g, :], ALU.mult, ALU.add)
                    ins.then_inc(u_ready, 1)
                    dve.wait_ge(u_ready, p + 1)
                    dve.wait_ge(eu_ready, since(p))
                    nc.vector.tensor_scalar(umin, u_sb, 0.0, None, ALU.min).then_inc(umin_ready, 1)

                def step(p, b, lag=2, norms=True, last=False):
                    if lag >= 2:
                        gather(p - 2, b)
                    if norms:
                        ahead, step_sem, ready_sem = p + 3, dstep, stats_ready
                        dve.wait_ge(xn_ready, p + 2)
                    else:
                        ahead, step_sem, ready_sem = p + 3 - PAIRS, l2_step, l2_stats_ready
                        if last:
                            dve.wait_ge(l2_xn_ready, 1)
                        else:
                            dve.wait_ge(xn_ready, p + 2)
                    moments(dve, ahead, step_sem, 1 - b)
                    if lag >= 1:
                        copy_pT(p - 1)
                    if lag >= 2:
                        elu_max(p - 2)
                    leaky(p)
                    mean_variance(dve, ahead, step_sem, 1 - b)
                    mask(p)
                    root_argument(dve, ahead, step_sem, ready_sem, 1 - b)
                    maximum(p)

                step(0, 0, lag=0)
                step(1, 1, lag=1)
                step(2, 0)
                step(3, 1)
                with dve.Fori(1, PAIRS // 4 - 1) as j:
                    for i in range(4):
                        step(4 * j + i, i % 2)
                for p in range(PAIRS - 4, PAIRS):
                    step(p, p % 2, norms=p + 3 < PAIRS, last=p == PAIRS - 1)
                gather(PAIRS - 2, 0)
                copy_pT(PAIRS - 1)
                elu_max(PAIRS - 2)
                dve.wait_ge(l2_high_ready, 1)
                nc.vector.tensor_tensor(yT_low[0], HT[:, :], yT_high[0].bitcast(F32), ALU.subtract).then_inc(l2_yt_ready, 1)
                gather(PAIRS - 1, 1)
                dve.wait_ge(l2_high_ready, 2)
                nc.vector.tensor_tensor(yT_low[1], HG[0][:, :], yT_high[1].bitcast(F32), ALU.subtract).then_inc(l2_yt_ready, 1)
                elu_max(PAIRS - 1)

            xn_ready, yt_done, dstep = l2_xn_ready, l2_yt_done, l2_step
            yt_ready, out_done = l2_yt_ready, sem("l2_out_done")
            bias_done, x_done = sem("l2_bias_done"), sem("l2_x_done")
            l2_x_done = x_done
            stats_ready, rstd_ready, shift_ready = l2_stats_ready, l2_rstd_ready, l2_shift_ready
            high_ready = l2_high_ready
            YT, OO, TQ = bank[0:2], bank[2:4], bank[7]
            xnb = [xn, xn2]

            @block.tensor
            def _(pe):
                def gather(p, b):
                    pe.wait_ge(yt_ready, since(p - 1))
                    gather_nodes(pe, YT[b], p, xnb[b], xn_ready).then_inc(yt_done, 1)

                def outputs(p, b):
                    pe.wait_ge(yt_ready, p + 1)
                    pe.wait_ge(x_done, since(p - 1))
                    for g in range(2):
                        ins = split_product(OO[b][:, g * D:(g + 1) * D], lambda k, c: yTs[b][k][:, c, g, :],
                                            lambda k, c: w2[k][:, c, :])
                    ins.then_inc(out_done, 1)

                pe.wait_ge(val_ready, PAIRS)
                pe.wait_ge(l1_pt_ready, PAIRS)
                for p in range(1, 4):
                    if p > 1:
                        gather(p, p % 2)
                    outputs(p - 1, (p - 1) % 2)
                with pe.Fori(1, PAIRS // 4) as j:
                    for i in range(4):
                        gather(4 * j + i, i % 2)
                        outputs(4 * j + i - 1, (i + 1) % 2)
                pe.wait_ge(l3_xn_ready, 1)
                transposes(TQ).then_inc(l3_tr_done, 1)
                outputs(PAIRS - 1, 1)

            @block.scalar
            def _(act):
                def normalise(p, b):
                    act.wait_ge(yt_done, since(p - 1))
                    relu_norm(act, p, b, xnb[b], shift_ready).then_inc(xn_ready, 1)

                def copy_high(p, b):
                    act.wait_ge(yt_done, p + 1)
                    act.wait_ge(out_done, since(p - 1))
                    nc.scalar.copy(yT_high[b], YT[b][:, :]).then_inc(high_ready, 1)

                normalise(3, 1)
                with act.Fori(0, PAIRS // 4 - 1) as j:
                    for i in range(4):
                        copy_high(4 * j + 2 + i, i % 2)
                        normalise(4 * j + 4 + i, i % 2)
                copy_high(PAIRS - 2, 0)
                copy_high(PAIRS - 1, 1)
                act.wait_ge(l3_tr_done, 1)
                nc.scalar.activation(hT_high, TQ[:, :], ACT.Relu).then_inc(l3_high_ready, 1)

            @block.gpsimd
            def _(pool):
                def add_bias(p):
                    pool.wait_ge(xn_ready, p + 1)
                    nc.gpsimd.tensor_tensor(x_pair(p), x_pair(p), rows[:, 0:1, :].to_broadcast([128, 2, D]),
                                            ALU.add).then_inc(bias_done, 1)

                add_bias(0)
                root_and_shift(pool, 3, stats_ready, rstd_ready, shift_ready, 1)
                add_bias(1)
                with pool.Fori(1, PAIRS // 4) as j:
                    for i in range(4):
                        root_and_shift(pool, 4 * j + i, stats_ready, rstd_ready, shift_ready, i % 2)
                        add_bias(4 * j + i - 2)
                inverse_root(pool, 0, l3_stats_ready, l3_rstd_ready)
                add_bias(PAIRS - 2)
                add_bias(PAIRS - 1)
                inverse_root(pool, 1, l3_stats_ready, l3_rstd_ready)

            @block.vector
            def _(dve):
                def low_part(p, b):
                    dve.wait_ge(high_ready, p + 1)
                    nc.vector.tensor_tensor(yT_low[b], YT[b][:, :], yT_high[b].bitcast(F32), ALU.subtract).then_inc(yt_ready, 1)

                def update(p, b):
                    dve.wait_ge(out_done, p + 1)
                    dve.wait_ge(bias_done, p + 1)
                    nc.vector.tensor_tensor(x_pair(p), OO[b][:, :].rearrange("p (g d) -> p g d", g=2), x_pair(p),
                                            ALU.add).then_inc(x_done, 1)

                def step(p, b, first=False, norms=True):
                    if norms:
                        dve.wait_ge(xn_ready, p + 2)
                        moments(dve, p + 3, dstep, 1 - b)
                    if not first:
                        low_part(p, b)
                    if norms:
                        mean_variance(dve, p + 3, dstep, 1 - b)
                    if not first:
                        update(p - 2, b)
                    if norms:
                        root_argument(dve, p + 3, dstep, stats_ready, 1 - b)

                step(0, 0, first=True)
                dve.wait_ge(l1_x_done, PAIRS)
                step(1, 1, first=True)
                step(2, 0)
                step(3, 1)
                with dve.Fori(1, PAIRS // 4 - 1) as j:
                    for i in range(4):
                        step(4 * j + i, i % 2)
                for p in range(PAIRS - 4, PAIRS):
                    step(p, p % 2, norms=p + 3 < PAIRS)
                    if p == PAIRS - 3:
                        dve.wait_ge(xn_ready, PAIRS - 1)
                        layer_norm_stats(dve, 0, l3_step, l3_stats_ready)
                    if p == PAIRS - 2:
                        dve.wait_ge(l3_rstd_ready, 1)
                        dve.wait_ge(yt_done, PAIRS - 1)
                        for g in range(2):
                            ins = nc.vector.tensor_scalar(xn[:, g, :], xs[:, g, :], mv[:, 0, g, 0:1], rstd[:, 0, g:g + 1],
                                                          ALU.subtract, ALU.mult)
                        ins.then_inc(l3_xn_ready, 1)
                dve.wait_ge(l3_high_ready, 1)
                nc.vector.scalar_tensor_tensor(hT_low, TQ[:, :], 0.0, hT_high.bitcast(F32), ALU.max,
                                               ALU.subtract).then_inc(l3_low_ready, 1)
                update(PAIRS - 2, 0)
                update(PAIRS - 1, 1)
                layer_norm_stats(dve, 1, l3_step, l3_stats_ready)

            xn_ready, tr_done, dstep = l3_xn_ready, l3_tr_done, l3_step
            q_done, q_ready, k_done, k_ready = sem("l3_q_done"), sem("l3_q_ready"), sem("l3_k_done"), sem("l3_k_ready")
            v_done, v_ready, s_done, s_masked = sem("l3_v_done"), sem("l3_v_ready"), sem("l3_s_done"), sem("l3_s_masked")
            high_ready, low_ready, o_high_ready = l3_high_ready, l3_low_ready, sem("l3_o_high_ready")
            nmax_ready, exp_done, rinv_ready = sem("l3_nmax_ready"), sem("l3_exp_done"), sem("l3_rinv_ready")
            prob_ready, pt_done, pt_ready = sem("l3_prob_ready"), sem("l3_pt_done"), sem("l3_pt_ready")
            o_done, o_ready, y_done, x_done = sem("l3_o_done"), sem("l3_o_ready"), sem("l3_y_done"), sem("l3_x_done")
            stats_ready, rstd_ready = l3_stats_ready, l3_rstd_ready
            bias_done, stored = sem("l3_bias_done"), sem("l3_stored")
            SS, PT, OT, TQ = bank[0:4], bank[4:6], bank[6], bank[7]
            VV, YY = PT
            KK = SS[3]
            nmax = [small[:, 8 * g:8 * g + 8] for g in range(2)]
            rsum = [small[:, 24 + 8 * g:32 + 8 * g] for g in range(2)]
            rinv = [small[:, 40 + 8 * g:48 + 8 * g] for g in range(2)]

            @block.tensor
            def _(pe):
                def turn(p):
                    pe.wait_ge(xn_ready, p + 1)
                    pe.wait_ge(q_ready, since(p))
                    transposes(TQ).then_inc(tr_done, 1)

                def project_q(p):
                    pe.wait_ge(low_ready, p + 1)
                    feature_product(TQ, wq3).then_inc(q_done, 1)

                def project_k(p):
                    pe.wait_ge(s_masked, 2 * R * p)
                    feature_product(KK, wk3).then_inc(k_done, 1)

                def project_v(t, g):
                    pe.wait_ge(pt_ready, since(2 * t - 3))
                    node_split_product(VV[:, 0:D], wv3, g).then_inc(v_done, 1)

                def scores(t, g):
                    for r in range(R):
                        pe.wait_ge(s_masked, since(R * t + r + 1 - R))
                        for c in range(C):
                            rows_r = slice(HD * r, HD * (r + 1))
                            ins = nc.tensor.matmul(SS[r][:, c * N:(c + 1) * N], qT[rows_r, c, g, :], kT[rows_r, c, g, :],
                                                   start=True, stop=True)
                        ins.then_inc(s_done, 1)

                def turn_prob(t, g, half, values=None, outputs=None):
                    pe.wait_ge(prob_ready, 2 * t + half + 1)
                    if half == 0:
                        pe.wait_ge(v_ready, values)
                    if outputs is not None:
                        pe.wait_ge(x_done, outputs)
                    for k in range(4):
                        ins = nc.tensor.transpose(PT[half][:, k * N:(k + 1) * N], prob[g][:, 4 * half + k, :], ident[:, :])
                    ins.then_inc(pt_done, 1)

                def attend(t, g):
                    pe.wait_ge(o_ready, since(t))
                    for half in range(2):
                        pe.wait_ge(pt_ready, 2 * t + half + 1)
                        for r in range(2 * half, 2 * half + 2):
                            for c in range(C):
                                h = c * R + r
                                ins = nc.tensor.matmul(OT[HD * r:HD * (r + 1), c * N:(c + 1) * N],
                                                       val[:, g, HD * h:HD * (h + 1)], probT[:, r * C + c, :], start=True, stop=True)
                    ins.then_inc(o_done, 1)

                def project_o(p):
                    pe.wait_ge(o_ready, 2 * p + 2)
                    for g in range(2):
                        ins = split_product(YY[:, g * D:(g + 1) * D], lambda k, c: oTs[k][:, g, c, :],
                                            lambda k, c: wo3[k][:, c, :])
                    ins.then_inc(y_done, 1)

                def pair(p, first=False, last=False):
                    pe.wait_ge(q_ready, p + 1)
                    pe.wait_ge(k_ready, p + 1)
                    scores(2 * p, 0)
                    if not first:
                        turn_prob(2 * p - 1, 1, 0, values=2 * p + 1)
                        turn_prob(2 * p - 1, 1, 1)
                    if not last:
                        turn(p + 1)
                    if not first:
                        attend(2 * p - 1, 1)
                    if first:
                        pe.wait_ge(v_ready, 1)
                    project_v(2 * p + 1, 1)
                    scores(2 * p + 1, 1)
                    if not first:
                        project_o(p - 1)
                    turn_prob(2 * p, 0, 0, values=2 * p + 2)
                    if not last:
                        project_q(p + 1)
                    turn_prob(2 * p, 0, 1, outputs=since(p))
                    if not last:
                        project_k(p + 1)
                    attend(2 * p, 0)
                    if not last:
                        project_v(2 * p + 2, 0)

                project_q(0)
                project_v(0, 0)
                pe.wait_ge(l2_x_done, PAIRS)
                project_k(0)
                pair(0, first=True)
                pair(1)
                with pe.Fori(2, PAIRS - 1) as p:
                    pair(p)
                pair(PAIRS - 1, last=True)
                turn_prob(2 * PAIRS - 1, 1, 0, values=2 * PAIRS)
                turn_prob(2 * PAIRS - 1, 1, 1)
                attend(2 * PAIRS - 1, 1)
                project_o(PAIRS - 1)

            @block.scalar
            def _(act):
                def relu_high(p):
                    act.wait_ge(tr_done, p + 1)
                    act.wait_ge(v_done, since(2 * p))
                    nc.scalar.activation(hT_high, TQ[:, :], ACT.Relu).then_inc(high_ready, 1)

                def copy_q(p):
                    act.wait_ge(q_done, p + 1)
                    for c in range(C):
                        ins = nc.scalar.activation(qT[:, c, :, :].rearrange("p g n -> p (g n)"), TQ[:, c * 2 * N:(c + 1) * 2 * N],
                                                   ACT.Identity, bias=bq[:, c:c + 1], scale=QSCALE)
                    ins.then_inc(q_ready, 1)

                def exponentials(t, g, half, start=0, end=4):
                    act.wait_ge(nmax_ready, 2 * t + half + 1)
                    for k in range(4 * half + start, 4 * half + end):
                        ins = nc.scalar.activation(prob[g][:, k, :], wide[g][:, k, :], ACT.Exp, bias=nmax[g][:, k:k + 1],
                                                   accum_out=rsum[g][:, k:k + 1])
                    if end == 4:
                        ins.then_inc(exp_done, 1)

                def copy_pT(t, half):
                    act.wait_ge(pt_done, 2 * t + half + 1)
                    act.wait_ge(o_done, since(t))
                    nc.scalar.copy(probT[:, 4 * half:4 * half + 4, :].rearrange("p r n -> p (r n)"),
                                   PT[half][:, :]).then_inc(pt_ready, 1)

                def copy_o(t, g):
                    act.wait_ge(o_done, t + 1)
                    nc.scalar.copy(oTs[0][:, g, :, :].rearrange("p c n -> p (c n)"), OT[:, 0:D]).then_inc(o_high_ready, 1)

                def pair(p, first=False, last=False):
                    if not first:
                        copy_pT(2 * p - 1, 0)
                        copy_pT(2 * p - 1, 1)
                    exponentials(2 * p, 0, 0, end=1)
                    if not first:
                        copy_o(2 * p - 1, 1)
                    exponentials(2 * p, 0, 0, start=1)
                    if not last:
                        relu_high(p + 1)
                    exponentials(2 * p, 0, 1)
                    exponentials(2 * p + 1, 1, 0, end=2)
                    copy_pT(2 * p, 0)
                    exponentials(2 * p + 1, 1, 0, start=2)
                    if not last:
                        copy_q(p + 1)
                    copy_pT(2 * p, 1)
                    exponentials(2 * p + 1, 1, 1)
                    copy_o(2 * p, 0)

                copy_q(0)
                pair(0, first=True)
                with act.Fori(1, PAIRS - 1) as p:
                    pair(p)
                pair(PAIRS - 1, last=True)
                copy_pT(2 * PAIRS - 1, 0)
                copy_pT(2 * PAIRS - 1, 1)
                copy_o(2 * PAIRS - 1, 1)

            @block.gpsimd
            def _(pool):
                def add_bias(p):
                    pool.wait_ge(xn_ready, p + 1)
                    nc.gpsimd.tensor_tensor(x_pair(p), x_pair(p), rows[:, 2:3, :].to_broadcast([128, 2, D]),
                                            ALU.add).then_inc(bias_done, 1)

                def divide(t, g, half):
                    pool.wait_ge(rinv_ready, 2 * t + half + 1)
                    heads = slice(4 * half, 4 * half + 4)
                    nc.gpsimd.tensor_tensor(prob[g][:, heads, :], prob[g][:, heads, :],
                                            rinv[g][:, heads].unsqueeze(2).to_broadcast([128, 4, N]),
                                            ALU.mult).then_inc(prob_ready, 1)

                def pair(p, norms=True, first=False):
                    if not first:
                        add_bias(p)
                    divide(2 * p, 0, 0)
                    divide(2 * p, 0, 1)
                    if first:
                        inverse_root(pool, 2, stats_ready, rstd_ready)
                    divide(2 * p + 1, 1, 0)
                    if norms:
                        inverse_root(pool, p + 3, stats_ready, rstd_ready)
                    divide(2 * p + 1, 1, 1)

                pair(0, first=True)
                add_bias(0)
                with pool.Fori(1, PAIRS - 3) as p:
                    pair(p)
                for p in range(PAIRS - 3, PAIRS):
                    pair(p, norms=False)

            @block.vector
            def _(dve):
                def normalise(p):
                    dve.wait_ge(rstd_ready, p + 1)
                    dve.wait_ge(tr_done, since(p))
                    for g in range(2):
                        ins = nc.vector.tensor_scalar(xn[:, g, :], x_of(p, g), mv[:, 0, g, 0:1], rstd[:, 0, g:g + 1],
                                                      ALU.subtract, ALU.mult)
                    ins.then_inc(xn_ready, 1)

                def copy_k(p):
                    dve.wait_ge(k_done, p + 1)
                    for c in range(C):
                        ins = nc.vector.tensor_scalar(kT[:, c, :, :].rearrange("p g n -> p (g n)"), KK[:, c * 2 * N:(c + 1) * 2 * N],
                                                      bk[:, c:c + 1], None, ALU.add)
                    ins.then_inc(k_ready, 1)

                def copy_v(t, g):
                    dve.wait_ge(v_done, t + 1)
                    nc.vector.tensor_tensor(val[:, g, 0:D], VV[:, 0:D], rows[:, 1, :], ALU.add).then_inc(v_ready, 1)

                def mask_max(t, g, half):
                    for r in range(2 * half, 2 * half + 2):
                        dve.wait_ge(s_done, R * t + r + 1)
                        nc.vector.tensor_tensor(wide[g][:, r * C:(r + 1) * C, :],
                                                SS[r][:, 0:C * N].rearrange("p (c n) -> p c n", c=C),
                                                mbias_pair, ALU.add).then_inc(s_masked, 1)
                    dve.wait_ge(s_masked, R * t + 2 * half + 2)
                    nc.vector.tensor_reduce(nmax[g][:, 4 * half:4 * half + 4], wide[g][:, 4 * half:4 * half + 4, :],
                                            AX_X, ALU.max, negate=True).then_inc(nmax_ready, 1)

                def inverse(t, g, half):
                    dve.wait_ge(exp_done, 2 * t + half + 1)
                    nc.vector.reciprocal(rinv[g][:, 4 * half:4 * half + 4],
                                         rsum[g][:, 4 * half:4 * half + 4]).then_inc(rinv_ready, 1)

                def low_h(p):
                    dve.wait_ge(high_ready, p + 1)
                    nc.vector.scalar_tensor_tensor(hT_low, TQ[:, :], 0.0, hT_high.bitcast(F32), ALU.max,
                                                   ALU.subtract).then_inc(low_ready, 1)

                def low_o(t, g):
                    dve.wait_ge(o_high_ready, t + 1)
                    nc.vector.tensor_tensor(oTs[1][:, g, :, :], OT[:, 0:D].rearrange("p (c n) -> p c n", c=C),
                                            oTs[0][:, g, :, :].bitcast(F32), ALU.subtract).then_inc(o_ready, 1)

                def update(p):
                    dve.wait_ge(y_done, p + 1)
                    dve.wait_ge(bias_done, p + 1)
                    nc.vector.tensor_tensor(x_pair(p), YY[:, :].rearrange("p (g d) -> p g d", g=2), x_pair(p),
                                            ALU.add).then_inc(x_done, 1)

                def pair(p, first=False, last=False, norms=True, normal=True):
                    mask_max(2 * p, 0, 0)
                    mask_max(2 * p, 0, 1)
                    if not first:
                        low_o(2 * p - 1, 1)
                    copy_v(2 * p + 1, 1)
                    inverse(2 * p, 0, 0)
                    mask_max(2 * p + 1, 1, 0)
                    if not last:
                        low_h(p + 1)
                    inverse(2 * p, 0, 1)
                    if first:
                        layer_norm_stats(dve, 2, dstep, stats_ready)
                    if not first:
                        update(p - 1)
                    mask_max(2 * p + 1, 1, 1)
                    inverse(2 * p + 1, 1, 0)
                    if normal:
                        normalise(p + 2)
                    if norms:
                        moments(dve, p + 3, dstep)
                    if not last:
                        copy_k(p + 1)
                    if norms:
                        mean_variance(dve, p + 3, dstep)
                        root_argument(dve, p + 3, dstep, stats_ready)
                    if not last:
                        copy_v(2 * p + 2, 0)
                    inverse(2 * p + 1, 1, 1)
                    low_o(2 * p, 0)

                copy_v(0, 0)
                normalise(1)
                copy_k(0)
                pair(0, first=True)
                with dve.Fori(1, PAIRS - 3) as p:
                    pair(p)
                pair(PAIRS - 3, norms=False)
                pair(PAIRS - 2, norms=False, normal=False)
                pair(PAIRS - 1, last=True, norms=False, normal=False)
                low_o(2 * PAIRS - 1, 1)
                update(PAIRS - 1)

            @block.sync
            def _(sp):
                with sp.Fori(0, PAIRS) as p:
                    sp.wait_ge(x_done, 1)
                    sp.wait_ge(x_done, p + 1)
                    sp.dma_start(out[bass.ds(2 * p, 2), :, :].rearrange("g n d -> n g d"), x_pair(p)).then_inc(stored, 16)
                sp.wait_ge(stored, 16 * PAIRS)


_INS = ["x", "adj", "L0_gnn_Wq", "L0_gnn_Wk", "L0_gnn_Wv", "L1_gnn_W", "L1_gnn_a", "L1_gnn_beta", "L2_gnn_weight",
        "L2_gnn_bias", "L3_gnn_Wq", "L3_gnn_bq", "L3_gnn_Wk", "L3_gnn_bk", "L3_gnn_Wv", "L3_gnn_bv", "L3_gnn_Wo", "L3_gnn_bo"]


def kernel(**inputs):
    import numpy as _np
    import concourse.bacc as _bacc
    from concourse import mybir as _mybir
    from concourse.bass_utils import run_bass_kernel_spmd as _run

    nc = _bacc.Bacc("TRN2", target_bir_lowering=False, num_devices=1)
    arrays, aps = {}, {}
    for name in _INS:
        a = _np.ascontiguousarray(inputs[name])
        arrays[f"in_{name}_dram"] = a
        aps[name] = nc.dram_tensor(f"in_{name}_dram", a.shape, _mybir.dt.from_np(a.dtype), kind="ExternalInput").ap()
    aps["out"] = nc.dram_tensor("out_0_dram", inputs["x"].shape, _mybir.dt.from_np(_np.dtype("float32")),
                                kind="ExternalOutput").ap()
    gnn_stack_kernel(nc, aps["x"], aps["adj"], aps)
    r = _run(nc, [arrays], core_ids=[0])
    return r.results[0]["out_0_dram"]
```
